# Optimizing a Trainium2 kernel written in Bass

```python
import numpy as np
import jax
import jax.numpy as jnp

def _softmax(x, axis=-1):
    return jax.nn.softmax(x, axis=axis)

def _gelu(x):
    return jax.nn.gelu(x, approximate=True)

def _silu(x):
    return jax.nn.silu(x)

def _sigmoid(x):
    return jax.nn.sigmoid(x)

def _layernorm(x, axis=-1, eps=1e-05):
    m = jnp.mean(x, axis=axis, keepdims=True)
    v = jnp.var(x, axis=axis, keepdims=True)
    return (x - m) / jnp.sqrt(v + eps)

def _scatter_add(tgt, idx, src, axis=0):
    return tgt.at[idx].add(src)

def _segment_sum(src, seg, n):
    return jax.ops.segment_sum(src, seg, n)
kernel_name = 'mk_gnn_ffn_d4_gnn_r16_923d71'

def setup_inputs(seed: int=0):
    np.random.seed(seed)
    _w = jnp.asarray

    def _rec_inputs():
        import jax
        import jax.numpy as jnp
        _gk = jax.random.key(seed)
        x = -0.0002117 + 1 * jax.random.normal(jax.random.fold_in(_gk, 1), (625, 512), jnp.float32)
        src = jax.random.randint(jax.random.fold_in(_gk, 2), (10000,), 0, 625, jnp.int32)
        dst = jnp.minimum((625 * jax.random.uniform(jax.random.fold_in(_gk, 3), (10000,)) ** 2.0).astype(jnp.int32), 9999)
        _o = jnp.argsort(dst, stable=True)
        src = src[_o]
        dst = dst[_o]
        edge_attr_128 = 0.000279952 + 1.00013 * jax.random.normal(jax.random.fold_in(_gk, 13), (10000, 128), jnp.float32)
        node_vec1 = jax.random.uniform(jax.random.fold_in(_gk, 15), (625, 1), jnp.float32, 0.0, 0.999957)
        return (x, src, dst, edge_attr_128, node_vec1)
    x, src, dst, edge_attr_128, node_vec1 = _rec_inputs()

    def _L0_gnn_setup():
        import jax, jax.numpy as jnp
        import numpy as np
        BN_EPS = 1e-05

        def batch_norm(h, gamma, beta):
            mu = jnp.mean(h, axis=0)
            var = jnp.var(h, axis=0)
            return (h - mu) * jax.lax.rsqrt(var + BN_EPS) * gamma + beta
        key = jax.random.key(seed)
        ks = jax.random.split(key, 6)
        N, E, dim = (3125, 100000, 512)
        hidden = dim * 2
        x = jax.random.normal(ks[0], (N, dim), dtype=jnp.float32)
        edge_index = jax.random.randint(ks[1], (2, E), 0, N, dtype=jnp.int64)
        s1 = 1.0 / np.sqrt(dim)
        s2 = 1.0 / np.sqrt(hidden)
        return {'x': x, 'edge_index': edge_index, 'eps': jnp.float32(0.0), 'W1': jax.random.uniform(ks[2], (dim, hidden), jnp.float32, -s1, s1), 'b1': jnp.zeros((hidden,), jnp.float32), 'g1': jnp.ones((hidden,), jnp.float32), 'be1': jnp.zeros((hidden,), jnp.float32), 'W2': jax.random.uniform(ks[3], (hidden, dim), jnp.float32, -s2, s2), 'b2': jnp.zeros((dim,), jnp.float32), 'g2': jnp.ones((dim,), jnp.float32), 'be2': jnp.zeros((dim,), jnp.float32)}
    _L0_gnn_all = _L0_gnn_setup()
    _L0_gnn_in = {k: v for k, v in _L0_gnn_all.items() if k in ('eps', 'W1', 'b1', 'g1', 'be1', 'W2', 'b2', 'g2', 'be2')}
    del _L0_gnn_all

    def _L0_ffn_setup():
        import jax, jax.numpy as jnp
        import numpy as np
        K = 2
        EPS = 1e-06

        def _layernorm(x, gamma, beta):
            mu = jnp.mean(x, axis=-1, keepdims=True)
            var = jnp.mean(jnp.square(x - mu), axis=-1, keepdims=True)
            return (x - mu) * jax.lax.rsqrt(var + EPS) * gamma + beta
        key = jax.random.key(seed)
        ks = jax.random.split(key, 5)
        B, S, D, F, E = (8, 128, 512, 128, 8)
        x = jax.random.normal(ks[0], (B, S, D), dtype=jnp.float32)
        router_w = jax.random.normal(ks[1], (D, E), dtype=jnp.float32) * 0.02
        w1 = jax.random.normal(ks[2], (E, D, F), dtype=jnp.float32) * 0.02
        b1 = jnp.zeros((E, F), dtype=jnp.float32)
        w2 = jax.random.normal(ks[3], (E, F, D), dtype=jnp.float32) * 0.02
        b2 = jnp.zeros((E, D), dtype=jnp.float32)
        gamma = jnp.ones((E, D), dtype=jnp.float32)
        beta = jnp.zeros((E, D), dtype=jnp.float32)
        return {'x': x, 'router_w': router_w, 'w1': w1, 'b1': b1, 'w2': w2, 'b2': b2, 'gamma': gamma, 'beta': beta}
    _L0_ffn_all = _L0_ffn_setup()
    _L0_ffn_in = {k: v for k, v in _L0_ffn_all.items() if k in ('router_w', 'w1', 'b1', 'w2', 'b2', 'gamma', 'beta')}
    del _L0_ffn_all

    def _L1_gnn_setup():
        import jax, jax.numpy as jnp
        import numpy as np
        N = 625
        E = 10000
        D = 512
        EDGE_DIM = 128
        L = 3
        LN_EPS = 1e-05
        key = jax.random.key(seed)
        ks = jax.random.split(key, 16)
        s = 0.02
        return {'x': jax.random.normal(ks[0], (N, D), dtype=jnp.float32), 'edge_index': jax.random.randint(ks[1], (2, E), 0, N, dtype=jnp.int64), 'edge_attr': jax.random.normal(ks[2], (E, EDGE_DIM), dtype=jnp.float32), 'We': jax.random.normal(ks[3], (L, EDGE_DIM, D), dtype=jnp.float32) * s, 'be': jnp.zeros((L, D), dtype=jnp.float32), 'eps': jnp.zeros((L,), dtype=jnp.float32), 'W1': jax.random.normal(ks[4], (L, D, D), dtype=jnp.float32) * s, 'b1': jnp.zeros((L, D), dtype=jnp.float32), 'W2': jax.random.normal(ks[5], (L, D, D), dtype=jnp.float32) * s, 'b2': jnp.zeros((L, D), dtype=jnp.float32), 'gamma': jnp.ones((L, D), dtype=jnp.float32), 'beta': jnp.zeros((L, D), dtype=jnp.float32), 'Wf': jax.random.normal(ks[6], (D, D), dtype=jnp.float32) * s, 'bf': jnp.zeros((D,), dtype=jnp.float32)}
    _L1_gnn_all = _L1_gnn_setup()
    _L1_gnn_in = {k: v for k, v in _L1_gnn_all.items() if k in ('We', 'be', 'eps', 'W1', 'b1', 'W2', 'b2', 'gamma', 'beta', 'Wf', 'bf')}
    del _L1_gnn_all

    def _L1_ffn_setup():
        import jax, jax.numpy as jnp
        import numpy as np
        EPS = 1e-09
        LN_EPS = 1e-05

        def _layernorm(x, gamma):
            x = x.astype(jnp.float32)
            mu = jnp.mean(x, axis=-1, keepdims=True)
            var = jnp.var(x, axis=-1, keepdims=True)
            return (x - mu) * jax.lax.rsqrt(var + LN_EPS) * gamma
        key = jax.random.key(seed)
        ks = jax.random.split(key, 5)
        b, n, d, e, h = (4, 1024, 512, 6, 128)
        x = jax.random.normal(ks[0], (b, n, d), dtype=jnp.float32)
        w_gating = jax.random.normal(ks[1], (d, e), dtype=jnp.float32)
        std1 = 1.0 / np.sqrt(h)
        std2 = 1.0 / np.sqrt(d)
        w1 = jax.random.uniform(ks[2], (e, d, h), jnp.float32, -std1, std1)
        w2 = jax.random.uniform(ks[3], (e, h, d), jnp.float32, -std2, std2)
        gamma = jnp.ones((d,), dtype=jnp.float32)
        return {'x': x, 'w_gating': w_gating, 'gamma': gamma, 'w1': w1, 'w2': w2}
    _L1_ffn_all = _L1_ffn_setup()
    _L1_ffn_in = {k: v for k, v in _L1_ffn_all.items() if k in ('w_gating', 'gamma', 'w1', 'w2')}
    del _L1_ffn_all

    def _L2_gnn_setup():
        import jax, jax.numpy as jnp
        import numpy as np
        N_NODES = 40962
        LATENT_DIM = 512
        N_EDGES = 40962
        NUM_BLOCKS = 4
        NUM_HEADS = 4
        NUM_FREQ = 32
        BASE_PERIOD = 16
        NOISE_EMB_DIM = 16
        EPS = 1e-05

        def _cond_layer_norm(x, cond, sw, sb, bw, bb):
            mu = jnp.mean(x, axis=-1, keepdims=True)
            var = jnp.var(x, axis=-1, keepdims=True)
            xn = (x - mu) * jax.lax.rsqrt(var + EPS)
            scale = cond @ sw + sb
            bias = cond @ bw + bb
            return xn * (1.0 + scale) + bias

        def _sparse_attention(x, src, dst, wq, bq, wk, bk, wv, bv, wo, bo):
            N, D = x.shape
            H, Dh = (NUM_HEADS, D // NUM_HEADS)
            q = (x @ wq + bq).reshape(N, H, Dh) * Dh ** (-0.5)
            k = (x @ wk + bk).reshape(N, H, Dh)
            v = (x @ wv + bv).reshape(N, H, Dh)
            scores = jnp.einsum('ehd,ehd->eh', q[src], k[dst])
            smax = jax.ops.segment_max(scores, src, num_segments=N)
            ex = jnp.exp(scores - smax[src])
            denom = jax.ops.segment_sum(ex, src, num_segments=N)
            attn = ex / denom[src]
            out = jax.ops.segment_sum(attn[:, :, None] * v[dst], src, num_segments=N)
            return out.reshape(N, D) @ wo + bo

        def _forward(x, edge_index, noise_levels, f_w1, f_b1, f_w2, f_b2, s1_w, s1_b, b1_w, b1_b, wq, bq, wk, bk, wv, bv, wo, bo, s2_w, s2_b, b2_w, b2_b, m_w1, m_b1, m_w2, m_b2):
            src, dst = (edge_index[0], edge_index[1])
            freqs = jnp.arange(1, NUM_FREQ + 1, dtype=x.dtype) * (2.0 * np.pi / BASE_PERIOD)
            ph = noise_levels * freqs
            emb = jnp.concatenate([jnp.sin(ph), jnp.cos(ph)], axis=-1)
            cond = jax.nn.silu(emb @ f_w1 + f_b1) @ f_w2 + f_b2
            for i in range(NUM_BLOCKS):
                y = _cond_layer_norm(x, cond, s1_w[i], s1_b[i], b1_w[i], b1_b[i])
                y = _sparse_attention(y, src, dst, wq[i], bq[i], wk[i], bk[i], wv[i], bv[i], wo[i], bo[i])
                x = x + y
                y = _cond_layer_norm(x, cond, s2_w[i], s2_b[i], b2_w[i], b2_b[i])
                y = jax.nn.relu(y @ m_w1[i] + m_b1[i]) @ m_w2[i] + m_b2[i]
                x = x + y
            return x
        key = jax.random.key(seed)
        ks = jax.random.split(key, 20)

        def w(k, shape, s=0.02):
            return jax.random.normal(k, shape, dtype=jnp.float32) * s
        D, B, C = (LATENT_DIM, NUM_BLOCKS, NOISE_EMB_DIM)
        z = lambda *s: jnp.zeros(s, jnp.float32)
        return {'latent_mesh_nodes': jax.random.normal(ks[0], (N_NODES, D), dtype=jnp.float32), 'edge_index': jax.random.randint(ks[1], (2, N_EDGES), 0, N_NODES, dtype=jnp.int32), 'noise_levels': jax.random.uniform(ks[2], (N_NODES, 1), dtype=jnp.float32), 'f_w1': w(ks[3], (2 * NUM_FREQ, C)), 'f_b1': z(C), 'f_w2': w(ks[4], (C, C)), 'f_b2': z(C), 's1_w': w(ks[5], (B, C, D)), 's1_b': z(B, D), 'b1_w': w(ks[6], (B, C, D)), 'b1_b': z(B, D), 'wq': w(ks[7], (B, D, D)), 'bq': z(B, D), 'wk': w(ks[8], (B, D, D)), 'bk': z(B, D), 'wv': w(ks[9], (B, D, D)), 'bv': z(B, D), 'wo': w(ks[10], (B, D, D)), 'bo': z(B, D), 's2_w': w(ks[11], (B, C, D)), 's2_b': z(B, D), 'b2_w': w(ks[12], (B, C, D)), 'b2_b': z(B, D), 'm_w1': w(ks[13], (B, D, D)), 'm_b1': z(B, D), 'm_w2': w(ks[14], (B, D, D)), 'm_b2': z(B, D)}
    _L2_gnn_all = _L2_gnn_setup()
    _L2_gnn_in = {k: v for k, v in _L2_gnn_all.items() if k in ('f_w1', 'f_b1', 'f_w2', 'f_b2', 's1_w', 's1_b', 'b1_w', 'b1_b', 'wq', 'bq', 'wk', 'bk', 'wv', 'bv', 'wo', 'bo', 's2_w', 's2_b', 'b2_w', 'b2_b', 'm_w1', 'm_b1', 'm_w2', 'm_b2')}
    del _L2_gnn_all

    def _L2_ffn_setup():
        import jax, jax.numpy as jnp
        import numpy as np
        B, T, C = (2, 128, 512)
        E, G, TG, K = (64, 8, 4, 6)
        H, HS = (160, 512)
        key = jax.random.key(seed)
        ks = jax.random.split(key, 9)
        s = 0.02
        return {'x': jax.random.normal(ks[0], (B, T, C), dtype=jnp.float32), 'router_w': jax.random.normal(ks[1], (E, C), dtype=jnp.float32) * s, 'bias_corr': jnp.zeros((E,), dtype=jnp.float32), 'Wg': jax.random.normal(ks[2], (E, C, H), dtype=jnp.float32) * s, 'Wu': jax.random.normal(ks[3], (E, C, H), dtype=jnp.float32) * s, 'Wd': jax.random.normal(ks[4], (E, H, C), dtype=jnp.float32) * s, 'sWg': jax.random.normal(ks[5], (C, HS), dtype=jnp.float32) * s, 'sWu': jax.random.normal(ks[6], (C, HS), dtype=jnp.float32) * s, 'sWd': jax.random.normal(ks[7], (HS, C), dtype=jnp.float32) * s}
    _L2_ffn_all = _L2_ffn_setup()
    _L2_ffn_in = {k: v for k, v in _L2_ffn_all.items() if k in ('router_w', 'bias_corr', 'Wg', 'Wu', 'Wd', 'sWg', 'sWu', 'sWd')}
    del _L2_ffn_all

    def _L3_gnn_setup():
        import jax, jax.numpy as jnp
        import numpy as np
        N = 3125
        E = 50000
        F_IN = 512
        F_OUT = 512
        key = jax.random.key(seed)
        k_feat, k_src, k_dst, k_w1, k_b1, k_w2, k_b2 = jax.random.split(key, 7)
        feat = jax.random.normal(k_feat, (N, F_IN), dtype=jnp.float32)
        src_idx = jax.random.randint(k_src, (E,), 0, N, dtype=jnp.int32)
        dst_idx = jax.random.randint(k_dst, (E,), 0, N, dtype=jnp.int32)
        deg = jax.ops.segment_sum(jnp.ones((E,), jnp.float32), dst_idx, num_segments=N)
        in_deg = jnp.maximum(deg, 1.0)
        stdv = 1.0 / np.sqrt(F_IN)
        W1 = jax.random.uniform(k_w1, (F_OUT, F_IN), jnp.float32, -stdv, stdv)
        b1 = jax.random.uniform(k_b1, (F_OUT,), jnp.float32, -stdv, stdv)
        W2 = jax.random.uniform(k_w2, (F_OUT, F_IN), jnp.float32, -stdv, stdv)
        b2 = jax.random.uniform(k_b2, (F_OUT,), jnp.float32, -stdv, stdv)
        return {'feat': feat, 'src_idx': src_idx, 'dst_idx': dst_idx, 'in_deg': in_deg, 'W1': W1, 'b1': b1, 'W2': W2, 'b2': b2}
    _L3_gnn_all = _L3_gnn_setup()
    _L3_gnn_in = {k: v for k, v in _L3_gnn_all.items() if k in ('W1', 'b1', 'W2', 'b2')}
    del _L3_gnn_all

    def _L3_ffn_setup():
        import jax, jax.numpy as jnp
        import numpy as np
        B, S, H, E, K = (8, 256, 512, 8, 2)
        key = jax.random.key(seed)
        ks = jax.random.split(key, 7)
        s_h = 1.0 / np.sqrt(H)
        s_2h = 1.0 / np.sqrt(2 * H)
        return {'x': jax.random.normal(ks[0], (B, S, H), dtype=jnp.float32), 'gate_w': jax.random.uniform(ks[1], (H, E), minval=-s_h, maxval=s_h, dtype=jnp.float32), 'gate_b': jax.random.uniform(ks[2], (E,), minval=-s_h, maxval=s_h, dtype=jnp.float32), 'w1': jax.random.uniform(ks[3], (E, H, 2 * H), minval=-s_h, maxval=s_h, dtype=jnp.float32), 'b1': jax.random.uniform(ks[4], (E, 2 * H), minval=-s_h, maxval=s_h, dtype=jnp.float32), 'w2': jax.random.uniform(ks[5], (E, 2 * H, H), minval=-s_2h, maxval=s_2h, dtype=jnp.float32), 'b2': jax.random.uniform(ks[6], (E, H), minval=-s_2h, maxval=s_2h, dtype=jnp.float32)}
    _L3_ffn_all = _L3_ffn_setup()
    _L3_ffn_in = {k: v for k, v in _L3_ffn_all.items() if k in ('gate_w', 'gate_b', 'w1', 'b1', 'w2', 'b2')}
    del _L3_ffn_all
    return {'x': x, 'src': src, 'dst': dst, 'edge_attr_128': edge_attr_128, 'node_vec1': node_vec1, 'L0_gnn_eps': _L0_gnn_in['eps'], 'L0_gnn_W1': _L0_gnn_in['W1'], 'L0_gnn_b1': _L0_gnn_in['b1'], 'L0_gnn_g1': _L0_gnn_in['g1'], 'L0_gnn_be1': _L0_gnn_in['be1'], 'L0_gnn_W2': _L0_gnn_in['W2'], 'L0_gnn_b2': _L0_gnn_in['b2'], 'L0_gnn_g2': _L0_gnn_in['g2'], 'L0_gnn_be2': _L0_gnn_in['be2'], 'L0_ffn_router_w': _L0_ffn_in['router_w'], 'L0_ffn_w1': _L0_ffn_in['w1'], 'L0_ffn_b1': _L0_ffn_in['b1'], 'L0_ffn_w2': _L0_ffn_in['w2'], 'L0_ffn_b2': _L0_ffn_in['b2'], 'L0_ffn_gamma': _L0_ffn_in['gamma'], 'L0_ffn_beta': _L0_ffn_in['beta'], 'L1_gnn_We': _L1_gnn_in['We'], 'L1_gnn_be': _L1_gnn_in['be'], 'L1_gnn_eps': _L1_gnn_in['eps'], 'L1_gnn_W1': _L1_gnn_in['W1'], 'L1_gnn_b1': _L1_gnn_in['b1'], 'L1_gnn_W2': _L1_gnn_in['W2'], 'L1_gnn_b2': _L1_gnn_in['b2'], 'L1_gnn_gamma': _L1_gnn_in['gamma'], 'L1_gnn_beta': _L1_gnn_in['beta'], 'L1_gnn_Wf': _L1_gnn_in['Wf'], 'L1_gnn_bf': _L1_gnn_in['bf'], 'L1_ffn_w_gating': _L1_ffn_in['w_gating'], 'L1_ffn_gamma': _L1_ffn_in['gamma'], 'L1_ffn_w1': _L1_ffn_in['w1'], 'L1_ffn_w2': _L1_ffn_in['w2'], 'L2_gnn_f_w1': _L2_gnn_in['f_w1'], 'L2_gnn_f_b1': _L2_gnn_in['f_b1'], 'L2_gnn_f_w2': _L2_gnn_in['f_w2'], 'L2_gnn_f_b2': _L2_gnn_in['f_b2'], 'L2_gnn_s1_w': _L2_gnn_in['s1_w'], 'L2_gnn_s1_b': _L2_gnn_in['s1_b'], 'L2_gnn_b1_w': _L2_gnn_in['b1_w'], 'L2_gnn_b1_b': _L2_gnn_in['b1_b'], 'L2_gnn_wq': _L2_gnn_in['wq'], 'L2_gnn_bq': _L2_gnn_in['bq'], 'L2_gnn_wk': _L2_gnn_in['wk'], 'L2_gnn_bk': _L2_gnn_in['bk'], 'L2_gnn_wv': _L2_gnn_in['wv'], 'L2_gnn_bv': _L2_gnn_in['bv'], 'L2_gnn_wo': _L2_gnn_in['wo'], 'L2_gnn_bo': _L2_gnn_in['bo'], 'L2_gnn_s2_w': _L2_gnn_in['s2_w'], 'L2_gnn_s2_b': _L2_gnn_in['s2_b'], 'L2_gnn_b2_w': _L2_gnn_in['b2_w'], 'L2_gnn_b2_b': _L2_gnn_in['b2_b'], 'L2_gnn_m_w1': _L2_gnn_in['m_w1'], 'L2_gnn_m_b1': _L2_gnn_in['m_b1'], 'L2_gnn_m_w2': _L2_gnn_in['m_w2'], 'L2_gnn_m_b2': _L2_gnn_in['m_b2'], 'L2_ffn_router_w': _L2_ffn_in['router_w'], 'L2_ffn_bias_corr': _L2_ffn_in['bias_corr'], 'L2_ffn_Wg': _L2_ffn_in['Wg'], 'L2_ffn_Wu': _L2_ffn_in['Wu'], 'L2_ffn_Wd': _L2_ffn_in['Wd'], 'L2_ffn_sWg': _L2_ffn_in['sWg'], 'L2_ffn_sWu': _L2_ffn_in['sWu'], 'L2_ffn_sWd': _L2_ffn_in['sWd'], 'L3_gnn_W1': _L3_gnn_in['W1'], 'L3_gnn_b1': _L3_gnn_in['b1'], 'L3_gnn_W2': _L3_gnn_in['W2'], 'L3_gnn_b2': _L3_gnn_in['b2'], 'L3_ffn_gate_w': _L3_ffn_in['gate_w'], 'L3_ffn_gate_b': _L3_ffn_in['gate_b'], 'L3_ffn_w1': _L3_ffn_in['w1'], 'L3_ffn_b1': _L3_ffn_in['b1'], 'L3_ffn_w2': _L3_ffn_in['w2'], 'L3_ffn_b2': _L3_ffn_in['b2']}

def reference(x, src, dst, edge_attr_128, node_vec1, L0_gnn_eps, L0_gnn_W1, L0_gnn_b1, L0_gnn_g1, L0_gnn_be1, L0_gnn_W2, L0_gnn_b2, L0_gnn_g2, L0_gnn_be2, L0_ffn_router_w, L0_ffn_w1, L0_ffn_b1, L0_ffn_w2, L0_ffn_b2, L0_ffn_gamma, L0_ffn_beta, L1_gnn_We, L1_gnn_be, L1_gnn_eps, L1_gnn_W1, L1_gnn_b1, L1_gnn_W2, L1_gnn_b2, L1_gnn_gamma, L1_gnn_beta, L1_gnn_Wf, L1_gnn_bf, L1_ffn_w_gating, L1_ffn_gamma, L1_ffn_w1, L1_ffn_w2, L2_gnn_f_w1, L2_gnn_f_b1, L2_gnn_f_w2, L2_gnn_f_b2, L2_gnn_s1_w, L2_gnn_s1_b, L2_gnn_b1_w, L2_gnn_b1_b, L2_gnn_wq, L2_gnn_bq, L2_gnn_wk, L2_gnn_bk, L2_gnn_wv, L2_gnn_bv, L2_gnn_wo, L2_gnn_bo, L2_gnn_s2_w, L2_gnn_s2_b, L2_gnn_b2_w, L2_gnn_b2_b, L2_gnn_m_w1, L2_gnn_m_b1, L2_gnn_m_w2, L2_gnn_m_b2, L2_ffn_router_w, L2_ffn_bias_corr, L2_ffn_Wg, L2_ffn_Wu, L2_ffn_Wd, L2_ffn_sWg, L2_ffn_sWu, L2_ffn_sWd, L3_gnn_W1, L3_gnn_b1, L3_gnn_W2, L3_gnn_b2, L3_ffn_gate_w, L3_ffn_gate_b, L3_ffn_w1, L3_ffn_b1, L3_ffn_w2, L3_ffn_b2):
    import jax
    import jax.numpy as jnp

    def _L0_gnn_ref(x, edge_index, eps, W1, b1, g1, be1, W2, b2, g2, be2):
        import jax, jax.numpy as jnp
        import numpy as np
        BN_EPS = 1e-05

        def batch_norm(h, gamma, beta):
            mu = jnp.mean(h, axis=0)
            var = jnp.var(h, axis=0)
            return (h - mu) * jax.lax.rsqrt(var + BN_EPS) * gamma + beta
        N = x.shape[0]
        src, dst = (edge_index[0], edge_index[1])
        agg = jax.ops.segment_sum(x[src], dst, num_segments=N)
        h = (1.0 + eps) * x + agg
        h = jax.nn.relu(batch_norm(h @ W1 + b1, g1, be1))
        h = h @ W2 + b2
        h = jax.nn.relu(batch_norm(h, g2, be2))
        return x + h

    def _L0_ffn_ref(x, router_w, w1, b1, w2, b2, gamma, beta):
        import jax, jax.numpy as jnp
        import numpy as np
        K = 2
        EPS = 1e-06

        def _layernorm(x, gamma, beta):
            mu = jnp.mean(x, axis=-1, keepdims=True)
            var = jnp.mean(jnp.square(x - mu), axis=-1, keepdims=True)
            return (x - mu) * jax.lax.rsqrt(var + EPS) * gamma + beta
        B, S, D = x.shape
        E = w1.shape[0]
        xf = x.reshape(-1, D)
        logits = xf @ router_w
        gate_vals, idx = jax.lax.top_k(logits, K)
        gates = jax.nn.softmax(gate_vals, axis=-1)
        out = jnp.zeros_like(xf)
        for e in range(E):
            h = jax.nn.relu(xf @ w1[e] + b1[e]) @ w2[e] + b2[e]
            y = _layernorm(xf + h, gamma[e], beta[e])
            w = jnp.sum(jnp.where(idx == e, gates, 0.0), axis=-1)
            out = out + w[:, None] * y
        return out.reshape(B, S, D)

    def _L1_gnn_ref(x, edge_index, edge_attr, We, be, eps, W1, b1, W2, b2, gamma, beta, Wf, bf):
        import jax, jax.numpy as jnp
        import numpy as np
        N = 625
        E = 10000
        D = 512
        EDGE_DIM = 128
        L = 3
        LN_EPS = 1e-05
        src = edge_index[0]
        dst = edge_index[1]
        n = x.shape[0]
        h = x
        for l in range(L):
            e = jax.nn.relu(h[src] + edge_attr @ We[l] + be[l])
            agg = jax.ops.segment_sum(e, dst, num_segments=n)
            g = (1.0 + eps[l]) * h + agg
            g = jax.nn.relu(g @ W1[l] + b1[l]) @ W2[l] + b2[l]
            g = jax.nn.relu(g)
            mu = jnp.mean(g, axis=-1, keepdims=True)
            var = jnp.mean(jnp.square(g - mu), axis=-1, keepdims=True)
            h = (g - mu) * jax.lax.rsqrt(var + LN_EPS) * gamma[l] + beta[l]
        return h @ Wf + bf

    def _L1_ffn_ref(x, w_gating, gamma, w1, w2):
        import jax, jax.numpy as jnp
        import numpy as np
        EPS = 1e-09
        LN_EPS = 1e-05

        def _layernorm(x, gamma):
            x = x.astype(jnp.float32)
            mu = jnp.mean(x, axis=-1, keepdims=True)
            var = jnp.var(x, axis=-1, keepdims=True)
            return (x - mu) * jax.lax.rsqrt(var + LN_EPS) * gamma
        b, n, d = x.shape
        E = w_gating.shape[-1]
        C = max(min(n, int(n * 6.0 / E)), 4)
        raw = jnp.einsum('bnd,de->bne', x, w_gating)
        probs = jax.nn.softmax(raw, axis=-1)
        gate1 = jnp.max(probs, axis=-1)
        idx1 = jnp.argmax(probs, axis=-1)
        mask1 = jax.nn.one_hot(idx1, E, dtype=jnp.float32)
        gates_wo1 = probs * (1.0 - mask1)
        gate2 = jnp.max(gates_wo1, axis=-1)
        denom = gate1 + gate2 + EPS
        gate1 = gate1 / denom
        pos1 = (jnp.cumsum(mask1, axis=-2) - mask1) * mask1
        mask1 = mask1 * (pos1 < float(C)).astype(jnp.float32)
        mask1_flat = jnp.sum(mask1, axis=-1)
        pos1_flat = jnp.sum(pos1, axis=-1).astype(jnp.int32)
        gate1 = gate1 * mask1_flat
        combine = gate1[..., None, None] * mask1_flat[..., None, None] * jax.nn.one_hot(idx1, E, dtype=jnp.float32)[..., None] * jax.nn.one_hot(pos1_flat, C, dtype=jnp.float32)[..., None, :]
        dispatch = (combine != 0).astype(jnp.float32)
        expert_in = jnp.einsum('bnd,bnec->ebcd', x, dispatch)
        xn = _layernorm(expert_in, gamma)
        hidden = jax.nn.gelu(jnp.einsum('ebcd,edh->ebch', xn, w1), approximate=False)
        expert_out = jnp.einsum('ebch,ehd->ebcd', hidden, w2)
        out = jnp.einsum('ebcd,bnec->bnd', expert_out, combine)
        return out

    def _L2_gnn_ref(latent_mesh_nodes, edge_index, noise_levels, f_w1, f_b1, f_w2, f_b2, s1_w, s1_b, b1_w, b1_b, wq, bq, wk, bk, wv, bv, wo, bo, s2_w, s2_b, b2_w, b2_b, m_w1, m_b1, m_w2, m_b2):
        import jax, jax.numpy as jnp
        import numpy as np
        N_NODES = 40962
        LATENT_DIM = 512
        N_EDGES = 40962
        NUM_BLOCKS = 4
        NUM_HEADS = 4
        NUM_FREQ = 32
        BASE_PERIOD = 16
        NOISE_EMB_DIM = 16
        EPS = 1e-05

        def _cond_layer_norm(x, cond, sw, sb, bw, bb):
            mu = jnp.mean(x, axis=-1, keepdims=True)
            var = jnp.var(x, axis=-1, keepdims=True)
            xn = (x - mu) * jax.lax.rsqrt(var + EPS)
            scale = cond @ sw + sb
            bias = cond @ bw + bb
            return xn * (1.0 + scale) + bias

        def _sparse_attention(x, src, dst, wq, bq, wk, bk, wv, bv, wo, bo):
            N, D = x.shape
            H, Dh = (NUM_HEADS, D // NUM_HEADS)
            q = (x @ wq + bq).reshape(N, H, Dh) * Dh ** (-0.5)
            k = (x @ wk + bk).reshape(N, H, Dh)
            v = (x @ wv + bv).reshape(N, H, Dh)
            scores = jnp.einsum('ehd,ehd->eh', q[src], k[dst])
            smax = jax.ops.segment_max(scores, src, num_segments=N)
            ex = jnp.exp(scores - smax[src])
            denom = jax.ops.segment_sum(ex, src, num_segments=N)
            attn = ex / denom[src]
            out = jax.ops.segment_sum(attn[:, :, None] * v[dst], src, num_segments=N)
            return out.reshape(N, D) @ wo + bo

        def _forward(x, edge_index, noise_levels, f_w1, f_b1, f_w2, f_b2, s1_w, s1_b, b1_w, b1_b, wq, bq, wk, bk, wv, bv, wo, bo, s2_w, s2_b, b2_w, b2_b, m_w1, m_b1, m_w2, m_b2):
            src, dst = (edge_index[0], edge_index[1])
            freqs = jnp.arange(1, NUM_FREQ + 1, dtype=x.dtype) * (2.0 * np.pi / BASE_PERIOD)
            ph = noise_levels * freqs
            emb = jnp.concatenate([jnp.sin(ph), jnp.cos(ph)], axis=-1)
            cond = jax.nn.silu(emb @ f_w1 + f_b1) @ f_w2 + f_b2
            for i in range(NUM_BLOCKS):
                y = _cond_layer_norm(x, cond, s1_w[i], s1_b[i], b1_w[i], b1_b[i])
                y = _sparse_attention(y, src, dst, wq[i], bq[i], wk[i], bk[i], wv[i], bv[i], wo[i], bo[i])
                x = x + y
                y = _cond_layer_norm(x, cond, s2_w[i], s2_b[i], b2_w[i], b2_b[i])
                y = jax.nn.relu(y @ m_w1[i] + m_b1[i]) @ m_w2[i] + m_b2[i]
                x = x + y
            return x
        return _forward(latent_mesh_nodes, edge_index, noise_levels, f_w1, f_b1, f_w2, f_b2, s1_w, s1_b, b1_w, b1_b, wq, bq, wk, bk, wv, bv, wo, bo, s2_w, s2_b, b2_w, b2_b, m_w1, m_b1, m_w2, m_b2)

    def _L2_ffn_ref(x, router_w, bias_corr, Wg, Wu, Wd, sWg, sWu, sWd):
        import jax, jax.numpy as jnp
        import numpy as np
        B, T, C = (2, 128, 512)
        E, G, TG, K = (64, 8, 4, 6)
        H, HS = (160, 512)
        Bx, Tx, Cx = x.shape
        S = Bx * Tx
        xf = x.reshape(S, Cx)
        shared = jax.nn.silu(xf @ sWg) * (xf @ sWu) @ sWd
        logits = xf.astype(jnp.float32) @ router_w.T
        scores = jax.nn.sigmoid(logits).astype(x.dtype)
        biased = scores + bias_corr
        epg = E // G
        group_scores = biased.reshape(S, G, epg).max(axis=-1)
        _, sel_g = jax.lax.top_k(group_scores, TG)
        rows = jnp.arange(S)[:, None]
        group_mask = jnp.zeros((S, G), dtype=x.dtype).at[rows, sel_g].set(1.0)
        expert_mask = jnp.repeat(group_mask, epg, axis=1)
        masked = jnp.where(expert_mask > 0, biased, -jnp.inf)
        _, topk_idx = jax.lax.top_k(masked, K)
        w = jnp.take_along_axis(scores, topk_idx, axis=1)
        w = w / (w.sum(axis=-1, keepdims=True) + 1e-20)
        combine = jnp.zeros((S, E), dtype=x.dtype).at[rows, topk_idx].add(w)
        g = jnp.einsum('sc,ech->seh', xf, Wg)
        u = jnp.einsum('sc,ech->seh', xf, Wu)
        h = jax.nn.silu(g) * u
        hw = combine[:, :, None] * h
        routed = jnp.einsum('seh,ehc->sc', hw, Wd)
        return (shared + routed).reshape(Bx, Tx, Cx)

    def _L3_gnn_ref(feat, src_idx, dst_idx, in_deg, W1, b1, W2, b2):
        import jax, jax.numpy as jnp
        import numpy as np
        N = 3125
        E = 50000
        F_IN = 512
        F_OUT = 512
        num_dst = in_deg.shape[0]
        agg = jax.ops.segment_sum(feat[src_idx], dst_idx, num_segments=num_dst)
        ah = agg / in_deg[:, None]
        out = jnp.einsum('nf,of->no', feat[:num_dst], W1) + b1 + jnp.einsum('nf,of->no', ah, W2) + b2
        return out

    def _L3_ffn_ref(x, gate_w, gate_b, w1, b1, w2, b2):
        import jax, jax.numpy as jnp
        import numpy as np
        B, S, H, E, K = (8, 256, 512, 8, 2)
        logits = jnp.einsum('bsh,he->bse', x, gate_w) + gate_b
        topk_vals, topk_idx = jax.lax.top_k(logits, K)
        topk_weights = jax.nn.softmax(topk_vals, axis=-1)
        mask = jax.nn.one_hot(topk_idx, E, dtype=topk_weights.dtype)
        weights = jnp.einsum('bske,bsk->bse', mask, topk_weights)
        h = jax.nn.relu(jnp.einsum('bsh,ehf->bsef', x, w1) + b1)
        expert_out = jnp.einsum('bsef,efh->bseh', h, w2) + b2
        return jnp.einsum('bseh,bse->bsh', expert_out, weights)
    edge_index = jnp.stack([src, dst])
    deg = jnp.maximum(jax.ops.segment_sum(jnp.ones(dst.shape, jnp.float32), dst, num_segments=625), 1.0)
    x = x + _L0_gnn_ref(_layernorm(x, axis=-1), edge_index, L0_gnn_eps, L0_gnn_W1, L0_gnn_b1, L0_gnn_g1, L0_gnn_be1, L0_gnn_W2, L0_gnn_b2, L0_gnn_g2, L0_gnn_be2)
    x = x + _L0_ffn_ref(_layernorm(x, axis=-1)[None], L0_ffn_router_w, L0_ffn_w1, L0_ffn_b1, L0_ffn_w2, L0_ffn_b2, L0_ffn_gamma, L0_ffn_beta)[0]
    x = x + _L1_gnn_ref(_layernorm(x, axis=-1), edge_index, edge_attr_128, L1_gnn_We, L1_gnn_be, L1_gnn_eps, L1_gnn_W1, L1_gnn_b1, L1_gnn_W2, L1_gnn_b2, L1_gnn_gamma, L1_gnn_beta, L1_gnn_Wf, L1_gnn_bf)
    x = x + _L1_ffn_ref(_layernorm(x, axis=-1)[None], L1_ffn_w_gating, L1_ffn_gamma, L1_ffn_w1, L1_ffn_w2)[0]
    x = x + _L2_gnn_ref(_layernorm(x, axis=-1), edge_index, node_vec1, L2_gnn_f_w1, L2_gnn_f_b1, L2_gnn_f_w2, L2_gnn_f_b2, L2_gnn_s1_w, L2_gnn_s1_b, L2_gnn_b1_w, L2_gnn_b1_b, L2_gnn_wq, L2_gnn_bq, L2_gnn_wk, L2_gnn_bk, L2_gnn_wv, L2_gnn_bv, L2_gnn_wo, L2_gnn_bo, L2_gnn_s2_w, L2_gnn_s2_b, L2_gnn_b2_w, L2_gnn_b2_b, L2_gnn_m_w1, L2_gnn_m_b1, L2_gnn_m_w2, L2_gnn_m_b2)
    x = x + _L2_ffn_ref(_layernorm(x, axis=-1)[None], L2_ffn_router_w, L2_ffn_bias_corr, L2_ffn_Wg, L2_ffn_Wu, L2_ffn_Wd, L2_ffn_sWg, L2_ffn_sWu, L2_ffn_sWd)[0]
    x = x + _L3_gnn_ref(_layernorm(x, axis=-1), src, dst, deg, L3_gnn_W1, L3_gnn_b1, L3_gnn_W2, L3_gnn_b2)
    x = x + _L3_ffn_ref(_layernorm(x, axis=-1)[None], L3_ffn_gate_w, L3_ffn_gate_b, L3_ffn_w1, L3_ffn_b1, L3_ffn_w2, L3_ffn_b2)[0]
    return x

_drawn_inputs = setup_inputs


def setup_inputs(seed=0):
    import zlib

    import numpy as np

    out = dict(_drawn_inputs(seed))
    spreads = {'L0_gnn_b1': (0.0, 2.0),
     'L0_gnn_g1': (1.0, 0.2),
     'L0_gnn_be1': (0.0, 0.268),
     'L0_gnn_b2': (0.0, 2.0),
     'L0_gnn_g2': (1.0, 0.2),
     'L0_gnn_be2': (0.0, 0.1),
     'L0_ffn_b1': (0.0, 0.8),
     'L0_ffn_b2': (0.0, 0.307),
     'L0_ffn_gamma': (1.0, 0.2),
     'L0_ffn_beta': (0.0, 0.319),
     'L1_gnn_be': (0.0, 0.284),
     'L1_gnn_eps': (0.0, 0.8),
     'L1_gnn_b1': (0.0, 0.626),
     'L1_gnn_b2': (0.0, 0.1),
     'L1_gnn_gamma': (1.0, 0.2),
     'L1_gnn_beta': (0.0, 0.327),
     'L1_gnn_bf': (0.0, 0.1),
     'L1_ffn_gamma': (1.0, 0.6),
     'L2_gnn_f_b1': (0.0, 0.8),
     'L2_gnn_f_b2': (0.0, 0.8),
     'L2_gnn_s1_b': (0.0, 0.8),
     'L2_gnn_b1_b': (0.0, 0.734),
     'L2_gnn_bq': (0.0, 0.8),
     'L2_gnn_bk': (0.0, 2.0),
     'L2_gnn_bv': (0.0, 0.335),
     'L2_gnn_bo': (0.0, 0.1),
     'L2_gnn_s2_b': (0.0, 0.8),
     'L2_gnn_b2_b': (0.0, 0.8),
     'L2_gnn_m_b1': (0.0, 0.526),
     'L2_gnn_m_b2': (0.0, 0.1),
     'L2_ffn_bias_corr': (0.0, 0.8)}
    factors = {'edge_attr_128': 6.323,
     'node_vec1': 8.0,
     'L0_ffn_w1': 3.63,
     'L0_ffn_w2': 2.967,
     'L1_gnn_We': 5.777,
     'L2_gnn_f_w1': 8.0,
     'L2_gnn_f_w2': 8.0,
     'L2_gnn_s1_w': 8.0,
     'L2_gnn_b1_w': 8.0,
     'L2_gnn_wq': 8.0,
     'L2_gnn_wk': 8.0,
     'L2_gnn_s2_w': 8.0,
     'L2_gnn_b2_w': 8.0,
     'L2_ffn_router_w': 8.0,
     'L2_ffn_Wg': 8.0,
     'L2_ffn_Wu': 8.0,
     'L2_ffn_Wd': 8.0,
     'L2_ffn_sWg': 4.687,
     'L2_ffn_sWu': 4.68,
     'L2_ffn_sWd': 4.616,
     'L3_gnn_b1': 24.996,
     'L3_gnn_b2': 24.5,
     'L3_ffn_gate_b': 48.921,
     'L3_ffn_b1': 64.0,
     'L3_ffn_b2': 48.034,
     'L3_gnn_W2': 3.25,
     'L3_ffn_gate_w': 3.501,
     'L3_ffn_w1': 4.407,
     'L3_ffn_w2': 3.462}
    for name, (base, spread) in spreads.items():
        noise = np.random.default_rng([zlib.crc32(name.encode()), seed]).standard_normal(out[name].shape)
        drawn = base * np.exp(spread * noise) if base else spread * noise
        out[name] = jnp.asarray(drawn.astype(out[name].dtype))
    for name, factor in factors.items():
        out[name] = (out[name] * factor).astype(out[name].dtype)
    return out
```

```python
import concourse.bass as bass
from concourse import mybir
from contextlib import ExitStack

F32 = mybir.dt.float32
BF16 = mybir.dt.bfloat16
I32 = mybir.dt.int32
U32 = mybir.dt.uint32
ALU = mybir.AluOpType
ACT = mybir.ActivationFunctionType
AX = mybir.AxisListType

N, E, D = 625, 10000, 512
R = 125
T = N // R
EC = E // R
HF = 313
NP = 2 * HF
KD = D // 128
NSLOT = 84
SLOT_UNROLL = 4
TINY, HUGE = 1e-30, 1e30
TWO_PI = 6.283185307179586


class Chain:

    def __init__(self, engine, sem):
        self.engine, self.sem, self.n = engine, sem, 0

    def mark(self, ins):
        ins.then_inc(self.sem, 1)
        self.n += 1

    def wait(self):
        self.engine.wait_ge(self.sem, self.n)

    def link(self, ins):
        self.mark(ins)
        self.wait()


class Ring:

    def __init__(self, readers, sems, slots):
        self.readers, self.sems, self.slots = readers, sems, slots

    def slot(self, j):
        return j % self.slots

    def wait_read(self, engine, j):
        who = self.readers[j]
        engine.wait_ge(self.sems[who], self.readers[:j + 1].count(who))

    def acquire(self, pe, j):
        if j >= self.slots:
            self.wait_read(pe, j - self.slots)


class Buffers:
    pass


def halves(columns):
    return columns.rearrange("p (a n) -> p a n", a=2)


def matmul_rows(nc, out, lhs, rhs, nk):
    for k in range(nk):
        last = nc.tensor.matmul(out, lhs(k), rhs(k), start=(k == 0), stop=(k == nk - 1))
    return last


def matmul_columns(nc, slot, m, lhs, rhs, nk):
    for k in range(nk):
        for a in range(2):
            last = nc.tensor.matmul(slot[0:m, a, 0:HF], lhs(k), rhs(k)[:, a * HF:(a + 1) * HF],
                                    start=(k == 0), stop=(k == nk - 1))
    return last


class Program:
    def __init__(self, nc, ctx, args):
        self.nc, self.ctx, self.args = nc, ctx, args
        self.open = []

    def sb(self, name, shape, dt=F32):
        return self.ctx.enter_context(self.nc.sbuf_tensor(name, shape, dt))

    def sems(self, *names):
        return [self.ctx.enter_context(self.nc.semaphore(n)) for n in names]


def layer_norm_dve(nc, dve, b, chain, s, src, dst, eps_col=0, pre=None):
    for t in range(T):
        chain.mark(nc.vector.bn_stats(b.stats[0:R, t, :], src[:, t, :]))
    chain.wait()
    for t in range(T):
        chain.mark(nc.vector.bn_aggr(b.mv[0:R, t, :], b.stats[0:R, t, :]))
    chain.wait()
    nc.vector.tensor_copy(b.var[0:R, 0:T], b.mv[0:R, :, 1]).then_inc(s["stats_ready"], 1)
    dve.wait_ge(s["std_ready"], 1)
    chain.link(nc.vector.reciprocal(b.rstd[0:R, 0:T], b.std[0:R, 0:T]))
    for t in range(T):
        nc.vector.tensor_scalar(dst[:, t, :], src[:, t, :], b.mv[0:R, t, 0:1], b.rstd[0:R, t:t + 1],
                                ALU.subtract, ALU.mult).then_inc(s["xn_ready"], 1)


def layer_norm_act(nc, act, b, s, eps):
    act.wait_ge(s["stats_ready"], 1)
    nc.scalar.activation(b.std[0:R, 0:T], b.var[0:R, 0:T], ACT.Sqrt, bias=eps).then_inc(s["std_ready"], 1)


def transposes_pe(nc, pe, b, s, src, ready, banks=(6, 7), identity=None):
    for t in range(T):
        if ready is not None:
            pe.wait_ge(ready, t + 1)
        if t >= 2:
            pe.wait_ge(s["xt_ready"], t - 1)
        for k in range(KD):
            last = nc.tensor.transpose(b.ps[:, banks[t % 2], k * R:(k + 1) * R],
                                       src[:, t, k * 128:(k + 1) * 128], b.ident[0:R, 0:R])
        last.then_inc(s["transposed"], 1)


def transposes_act(nc, act, b, s, dst, banks=(6, 7)):
    for t in range(T):
        act.wait_ge(s["transposed"], t + 1)
        nc.scalar.activation(dst[:, :, t * R:(t + 1) * R],
                             b.ps[:, banks[t % 2], 0:KD * R].rearrange("p (k n) -> p k n", k=KD),
                             ACT.Copy).then_inc(s["xt_ready"], 1)


def semaphores(p, tag, *names):
    ctx = ExitStack()
    by_name = {n: ctx.enter_context(p.nc.semaphore(f"{tag}_{n}")) for n in names}
    p.open.append((ctx, by_name))
    return by_name


def release_semaphores(nc, p):
    with nc.Block(no_gpsimd_drain=True) as block:
        @block.sync
        def _(sp):
            for _, by_name in p.open:
                for x in by_name.values():
                    sp.sem_clear(x)
    for ctx, _ in p.open:
        ctx.close()
    p.open = []


def wait_positive(engine, sem, value):
    if not (isinstance(value, int) and value <= 0):
        engine.wait_ge(sem, value)


def setup_block(nc, p, b, A):
    s = semaphores(p, "setup", "loaded", "ones_set", "pool_done", "converted")
    with nc.Block() as block:
        @block.sync
        def _(sp):
            sp.dma_start(b.X[0:R, :, :], A["x"].rearrange("p (t d) -> p t d", t=T)).then_inc(s["loaded"], 16)
            sp.dma_start(b.idx_int[0:R, 0, :], A["src"]).then_inc(s["loaded"], 16)
            sp.dma_start(b.idx_int[0:R, 1, :], A["dst"]).then_inc(s["loaded"], 16)
            sp.dma_start(b.cols[:, :], A["cols"]).then_inc(s["loaded"], 16)
            sp.wait_ge(s["loaded"], 64)

        @block.gpsimd
        def _(pool):
            nc.gpsimd.memset(b.ident[:, :], 0.0).then_inc(s["ones_set"], 1)
            nc.gpsimd.memset(b.tri[:, :], 1.0).then_inc(s["ones_set"], 1)
            pool.wait_ge(s["ones_set"], 2)
            nc.gpsimd.affine_select(out=b.ident[:, :], in_=b.ident[:, :], compare_op=ALU.not_equal, fill=1.0,
                                    base=0, pattern=[[-1, 128]], channel_multiplier=1).then_inc(s["pool_done"], 1)
            nc.gpsimd.affine_select(out=b.tri[:, :], in_=b.tri[:, :], compare_op=ALU.is_gt, fill=0.0,
                                    base=0, pattern=[[1, 128]], channel_multiplier=-1).then_inc(s["pool_done"], 1)
            nc.gpsimd.iota(b.iota_int[:, :], pattern=[[1, NP]], base=0, channel_multiplier=0).then_inc(s["pool_done"], 1)
            nc.gpsimd.iota(b.eid_int[:, :], pattern=[[1, EC]], base=0, channel_multiplier=EC).then_inc(s["pool_done"], 1)
            nc.gpsimd.memset(b.XT[:, :, :], 0.0).then_inc(s["pool_done"], 1)
            nc.gpsimd.memset(b.ones[:, :], 1.0).then_inc(s["pool_done"], 1)
            nc.gpsimd.memset(b.eps5[:, :], 1e-5).then_inc(s["pool_done"], 1)
            nc.gpsimd.memset(b.eps6[:, :], 1e-6).then_inc(s["pool_done"], 1)
            nc.gpsimd.memset(b.half_pi[:, :], TWO_PI / 4).then_inc(s["pool_done"], 1)

        @block.vector
        def _(dve):
            dve.wait_ge(s["loaded"], 64)
            nc.vector.tensor_copy(b.idx[0:R, :, :], b.idx_int[0:R, :, :]).then_inc(s["converted"], 1)
            dve.wait_ge(s["pool_done"], 9)
            nc.vector.tensor_copy(b.iota[:, :], b.iota_int[:, :]).then_inc(s["converted"], 1)
            nc.vector.tensor_copy(b.eid[:, :], b.eid_int[:, :]).then_inc(s["converted"], 1)


def count_block(nc, p, b, A):
    s = semaphores(p, "count", "src_hot", "dst_hot", "counted", "copied")
    ps = b.ps
    U = 4
    with nc.Block(no_gpsimd_drain=True) as block:
        passes = ((0, 3), (3, 2))

        @block.gpsimd
        def _(pool):
            pass

        @block.vector
        def _(dve):
            for n, (s0, ns) in enumerate(passes):
                def column(i, u):
                    j = i * U + u
                    done = n * EC + j
                    wait_positive(dve, s["counted"], done - U + 1)
                    nc.vector.tensor_scalar(b.src_hot[0:R, u, 0:ns * R], b.iota[0:R, s0 * R:(s0 + ns) * R],
                                            b.idx[0:R, 0, bass.ds(j, 1)], None, ALU.is_equal).then_inc(s["src_hot"], 1)
                    nc.vector.tensor_scalar(b.dst_hot[0:R, u, :], b.iota[0:R, :],
                                            b.idx[0:R, 1, bass.ds(j, 1)], None, ALU.is_equal).then_inc(s["dst_hot"], 1)

                for u in range(U):
                    column(0, u)
                with dve.Fori(1, EC // U) as i:
                    for u in range(U):
                        column(i, u)
                dve.wait_ge(s["counted"], (n + 1) * EC)
                for q in range(ns):
                    nc.vector.tensor_copy(halves(b.CNT[0:R, s0 + q, :]), ps[0:R, 2 * q:2 * q + 2, 0:HF])\
                        .then_inc(s["copied"], 1)

        @block.tensor
        def _(pe):
            for n, (s0, ns) in enumerate(passes):
                def column(i, u, start, stop):
                    j = n * EC + i * U + u
                    pe.wait_ge(s["dst_hot"], j + 1)
                    for q in range(ns):
                        for a in range(2):
                            last = nc.tensor.matmul(ps[0:R, 2 * q + a, 0:HF], b.src_hot[0:R, u, q * R:(q + 1) * R],
                                                    b.dst_hot[0:R, u, a * HF:(a + 1) * HF], start=start, stop=stop)
                    last.then_inc(s["counted"], 1)

                if n:
                    pe.wait_ge(s["copied"], passes[0][1])
                for u in range(U):
                    column(0, u, u == 0, False)
                with pe.Fori(1, EC // U - 1) as i:
                    for u in range(U):
                        column(i, u, False, False)
                for u in range(U):
                    column(EC // U - 1, u, False, u == U - 1)


def slots_block(nc, p, b, A, table):
    s = semaphores(p, "slots", "chain", "tiles_hot", "summed", "payload", "initial", "initial_in", "reloaded")
    scattered, = p.sems("slots_scattered")
    NB = T
    with nc.Block() as block:
        @block.sync
        def _(sp):
            sp.wait_ge(s["initial"], 2)
            sp.dma_start(table.rearrange("(t q) c -> q t c", q=128), b.slot_init[:, :, :]).then_inc(s["initial_in"], 16)
            sp.wait_ge(scattered, 16 * EC)
            sp.dma_start(b.slot_tab[:, :, :], table.rearrange("(t q) c -> q t c", q=128)).then_inc(s["reloaded"], 16)
            sp.wait_ge(s["reloaded"], 16)

        @block.gpsimd
        def _(pool):
            nc.gpsimd.memset(b.slot_init[:, :, :], 0.0).then_inc(s["initial"], 1)
            pool.wait_ge(s["initial"], 1)
            nc.gpsimd.memset(b.slot_init[:, :, 1:2], -1.0).then_inc(s["initial"], 1)
            pool.wait_ge(s["initial_in"], 16)
            pool.wait_ge(s["payload"], 1)
            for j in range(EC):
                nc.gpsimd.indirect_dma_start(table, bass.IndirectOffsetOnAxis(ap=b.place[0:R, j:j + 1], axis=0),
                                             b.payload[0:R, j, :], None).then_inc(scattered, 16)

        @block.tensor
        def _(pe):
            pe.wait_ge(s["tiles_hot"], 1)
            hot = b.tile_hot[0:R, :, :].rearrange("p k j -> p (k j)")
            nc.tensor.matmul(b.ps[0:R, 0, 0:NB * EC], b.tri[0:R, 0:R], hot, start=True, stop=True)
            nc.tensor.matmul(b.ps[0:R, 1, 0:NB * EC], b.ones[0:R, 0:R], hot, start=True, stop=True)\
                .then_inc(s["summed"], 1)

        @block.vector
        def _(dve):
            c = Chain(dve, s["chain"])
            v = nc.vector
            dst, src = b.idx[0:R, 1, :], b.idx[0:R, 0, :]
            ge, hot = b.tile_ge[0:R, :, :], b.tile_hot[0:R, :, :]
            for k in range(NB):
                c.mark(v.tensor_scalar(ge[:, k, :], dst, float(R * k), None, ALU.is_ge))
            c.wait()
            c.mark(v.tensor_tensor(hot[:, 0:NB - 1, :], ge[:, 0:NB - 1, :], ge[:, 1:NB, :], ALU.subtract))
            c.link(v.tensor_copy(hot[:, NB - 1, :], ge[:, NB - 1, :]))
            nc.vector.tensor_copy(b.slot_tmp[0:R, 0, :], dst).then_inc(s["tiles_hot"], 1)
            dve.wait_ge(s["tiles_hot"], 1)
            for k in range(1, NB):
                c.link(v.scalar_tensor_tensor(b.slot_tmp[0:R, 0, :], ge[:, k, :], -float(R), b.slot_tmp[0:R, 0, :],
                                              ALU.mult, ALU.add))
            c.mark(v.memset(b.payload[0:R, :, :], 0.0))
            c.wait()
            c.mark(v.tensor_copy(b.payload[0:R, :, 0], src))
            c.mark(v.tensor_copy(b.payload[0:R, :, 1], b.slot_tmp[0:R, 0, :]))
            c.mark(v.tensor_copy(b.payload[0:R, :, 2], b.eid[0:R, :]))
            dve.wait_ge(s["summed"], 1)
            below = b.ps[0:R, 0, 0:NB * EC].rearrange("p (k j) -> p k j", k=NB)
            colsum = b.ps[0:R, 1, 0:NB * EC].rearrange("p (k j) -> p k j", k=NB)
            now, new = b.scan_a[0:R, :, :], b.scan_b[0:R, :, :]
            c.link(v.tensor_copy(now, colsum))
            step = 1
            while step < EC:
                c.mark(v.tensor_tensor(new[:, :, step:], now[:, :, step:], now[:, :, :EC - step], ALU.add))
                c.link(v.tensor_copy(new[:, :, :step], now[:, :, :step]))
                now, new = new, now
                step *= 2
            c.link(v.tensor_scalar(b.few[0:R, 0, :], now[:, :, EC - 1], 127.0, None, ALU.add))
            c.link(v.tensor_copy(b.few_int[0:R, 0, :], b.few[0:R, 0, :]))
            c.link(v.tensor_scalar(b.few_int[0:R, 1, :], b.few_int[0:R, 0, :], 7, None, ALU.arith_shift_right))
            c.link(v.tensor_copy(b.few[0:R, 1, :], b.few_int[0:R, 1, :]))
            c.mark(v.memset(b.few[0:R, 2, 0:1], 0.0))
            c.link(v.tensor_copy(b.few[0:R, 3, 0:1], b.few[0:R, 1, 0:1]))
            for k in range(1, NB):
                c.mark(v.tensor_copy(b.few[0:R, 2, k:k + 1], b.few[0:R, 3, k - 1:k]))
                c.link(v.tensor_tensor(b.few[0:R, 3, k:k + 1], b.few[0:R, 3, k - 1:k], b.few[0:R, 1, k:k + 1],
                                       ALU.add))
            c.link(v.tensor_scalar(b.few[0:R, 4, :], b.few[0:R, 2, :], 128.0, None, ALU.mult))
            c.link(v.tensor_tensor(new, now, colsum, ALU.subtract))
            c.link(v.tensor_tensor(now, new, below, ALU.add))
            for k in range(NB):
                c.link(v.scalar_tensor_tensor(new[:, k, :], now[:, k, :], b.few[0:R, 4, k:k + 1], hot[:, k, :],
                                              ALU.add, ALU.mult))
            for k in range(1, NB):
                c.link(v.tensor_tensor(new[:, 0, :], new[:, 0, :], new[:, k, :], ALU.add))
            nc.vector.tensor_copy(b.place[0:R, :], new[:, 0, :]).then_inc(s["payload"], 1)
            c.link(v.memset(b.slot_tile[0:R, :], 0.0))
            for k in range(NB):
                c.link(v.scalar_tensor_tensor(b.slot_tile[0:R, :], b.iota[0:R, 0:NSLOT], b.few[0:R, 3, k:k + 1],
                                              b.slot_tile[0:R, :], ALU.is_ge, ALU.add))
            c.link(v.tensor_scalar(b.slot_tile[0:R, :], b.slot_tile[0:R, :], float(NB - 1), float(D),
                                   ALU.min, ALU.mult))
            c.mark(v.tensor_copy(b.slot_off[0:R, :], b.slot_tile[0:R, :]))
            dve.wait_ge(s["reloaded"], 16)
            c.mark(v.tensor_copy(b.slot_src[:, :], b.slot_tab[:, :, 0]))
            c.mark(v.tensor_copy(b.slot_edge[:, :], b.slot_tab[:, :, 2]))
            c.mark(v.tensor_copy(b.slot_dst[:, :], b.slot_tab[:, :, 1]))


def attributes_block(nc, p, b, A):
    s = semaphores(p, "attr", "slot_begun", "idx_copied", "transposed", "stored")
    arrived = p.sems("attr_in0", "attr_in1", "attr_in2", "attr_in3")
    U = SLOT_UNROLL
    turns = NSLOT // U
    with nc.Block() as block:
        @block.gpsimd
        def _(pool):
            def turn(i, first):
                for u in range(U):
                    t = i * U + u
                    if not first:
                        pool.wait_ge(arrived[u], 16 * i)
                    nc.gpsimd.tensor_copy(b.gather_idx[u][:, :], b.slot_edge[:, bass.ds(t, 1)])\
                        .then_inc(s["idx_copied"], 1)
                    pool.wait_ge(s["idx_copied"], t + 1)
                    pool.sem_inc(s["slot_begun"], 1)
                    if not first:
                        pool.wait_ge(s["transposed"], t - U + 1)
                        pool.sem_inc(s["slot_begun"], 1)
                    nc.gpsimd.indirect_dma_start(
                        b.gathered[u][:, 0:128], None, A["edge_attr_128"],
                        bass.IndirectOffsetOnAxis(ap=b.gather_idx[u][:, 0:1], axis=0)).then_inc(arrived[u], 16)

            turn(0, True)
            with pool.Fori(1, turns) as i:
                turn(i, False)

        @block.tensor
        def _(pe):
            def turn(i):
                for u in range(U):
                    t = i * U + u
                    pe.wait_ge(arrived[u], 16 * (i + 1))
                    wait_positive(pe, s["stored"], t - 1)
                    nc.tensor.transpose(b.ps[:, u % 2, 0:128], b.gathered[u][:, 0:128], b.ident[:, :])\
                        .then_inc(s["transposed"], 1)

            turn(0)
            with pe.Fori(1, turns) as i:
                turn(i)

        @block.vector
        def _(dve):
            with dve.Fori(0, turns) as i:
                for u in range(U):
                    t = i * U + u
                    dve.wait_ge(s["transposed"], t + 1)
                    nc.vector.tensor_scalar(b.EAT[:, bass.ds(t * 128, 128)], b.ps[:, u % 2, 0:128], 1.0, None,
                                            ALU.mult).then_inc(s["stored"], 1)


def l0_gnn_block(nc, p, b, A):
    s = semaphores(p, "g0", "chain", "loaded", "stats_ready", "std_ready", "xn_ready", "eps_ready", "cnt_ready",
             "mm", "act", "dve", "bn_var", "bn_std", "bn_affine", "bn_done", "sum_ready", "out_t")
    ring = Ring(["act"] * 16, {"act": s["act"]}, 4)
    H1, H2 = 2 * D // 128, D // 128
    W1 = b.W[:, 0:4096].rearrange("p (k n) -> p k n", k=KD)
    W2 = b.W[:, 4096:8192].rearrange("p (k n) -> p k n", k=H1)
    C = b.col_of
    with nc.Block(no_gpsimd_drain=True) as block:
        @block.sync
        def _(sp):
            sp.dma_start(b.eps_col[0:R, :], A["L0_gnn_eps"].partition_broadcast(R)).then_inc(s["eps_ready"], 16)
            sp.dma_start(b.W[:, 0:4096], A["L0_gnn_W1"]).then_inc(s["loaded"], 16)
            sp.dma_start(b.W[:, 4096:8192], A["L0_gnn_W2"]).then_inc(s["loaded"], 16)

        @block.gpsimd
        def _(pool):
            for t in range(T):
                pool.wait_ge(s["xn_ready"], t + 1)
                nc.gpsimd.tensor_tensor(b.H[0:R, t, :], b.X[0:R, t, :], b.XN[0:R, t, :], ALU.add)\
                    .then_inc(s["sum_ready"], 1)

        @block.vector
        def _(dve):
            c = Chain(dve, s["chain"])
            v = nc.vector
            layer_norm_dve(nc, dve, b, c, s, b.X[0:R, :, :], b.XN[0:R, :, :])
            dve.wait_ge(s["eps_ready"], 16)
            c.link(v.tensor_scalar(b.eps_col[0:R, :], b.eps_col[0:R, :], 1.0, None, ALU.add))
            c.link(v.tensor_copy(b.P[0:R, :, :], b.CNT[0:R, :, :]))
            for t in range(T):
                v.scalar_tensor_tensor(b.P[0:R, t, t * R:(t + 1) * R], b.ident[0:R, 0:R], b.eps_col[0:R, 0:1],
                                       b.CNT[0:R, t, t * R:(t + 1) * R], ALU.mult, ALU.add).then_inc(s["cnt_ready"], 1)

            def batch_norm(buf, nm, g, be, done_jobs, n):
                for m in range(nm):
                    dve.wait_ge(s["act"], done_jobs + m + 1)
                    c.mark(v.bn_stats(b.bn_st[:, m, 0, :], buf[:, m, 0:HF]))
                    c.link(v.bn_stats(b.bn_st[:, m, 1, :], buf[:, m, HF:N]))
                    c.link(v.bn_aggr(b.bn_mv[:, m, :], b.bn_st[:, m, :, :].rearrange("p a c -> p (a c)")))
                v.tensor_copy(b.bn_var[:, 0:nm], b.bn_mv[:, 0:nm, 1]).then_inc(s["bn_var"], 1)
                dve.wait_ge(s["bn_std"], n)
                c.link(v.reciprocal(b.bn_scale[:, 0:nm], b.bn_std[:, 0:nm]))
                c.link(v.tensor_tensor(b.bn_scale[:, 0:nm], b.bn_scale[:, 0:nm], b.cols[:, g:g + nm], ALU.mult))
                c.link(v.tensor_tensor(b.bn_bias[:, 0:nm], b.bn_scale[:, 0:nm], b.bn_mv[:, 0:nm, 0], ALU.mult))
                v.tensor_tensor(b.bn_bias[:, 0:nm], b.cols[:, be:be + nm], b.bn_bias[:, 0:nm], ALU.subtract)\
                    .then_inc(s["bn_affine"], 1)

            batch_norm(b.HT, H1, C["g1"], C["be1"], H2, 1)
            batch_norm(b.QT, H2, C["g2"], C["be2"], H2 + H1, 2)
            for t in range(T):
                dve.wait_ge(s["out_t"], t + 1)
                dve.wait_ge(s["sum_ready"], t + 1)
                v.tensor_tensor(b.X[0:R, t, :], b.H[0:R, t, :], b.ps[0:R, t % 4, :], ALU.add).then_inc(s["dve"], 1)

        @block.tensor
        def _(pe):
            for m in range(H2):
                if m == 0:
                    pe.wait_ge(s["xn_ready"], T)
                    pe.wait_ge(s["cnt_ready"], T)
                ring.acquire(pe, m)
                matmul_columns(nc, b.slot(ring.slot(m)), 128, lambda k: b.XN[0:R, k, m * 128:(m + 1) * 128],
                               lambda k: b.P[0:R, k, :], T).then_inc(s["mm"], 1)
            pe.wait_ge(s["loaded"], 32)
            for m in range(H1):
                ring.acquire(pe, H2 + m)
                if m == 0:
                    ring.wait_read(pe, H2 - 1)
                matmul_columns(nc, b.slot(ring.slot(H2 + m)), 128, lambda k: W1[:, k, m * 128:(m + 1) * 128],
                               lambda k: b.XT[:, k, :], KD).then_inc(s["mm"], 1)
            pe.wait_ge(s["bn_done"], H1)
            for m in range(H2):
                ring.acquire(pe, H2 + H1 + m)
                matmul_columns(nc, b.slot(ring.slot(H2 + H1 + m)), 128, lambda k: W2[:, k, m * 128:(m + 1) * 128],
                               lambda k: b.HT[:, k, :], H1).then_inc(s["mm"], 1)
            pe.wait_ge(s["bn_done"], H1 + H2)
            for t in range(T):
                if t >= 4:
                    pe.wait_ge(s["dve"], t - 3)
                for k in range(KD):
                    last = nc.tensor.transpose(b.ps[0:R, t % 4, k * 128:(k + 1) * 128],
                                               b.QT[:, k, t * R:(t + 1) * R], b.ident[:, :])
                last.then_inc(s["out_t"], 1)

        @block.scalar
        def _(act):
            layer_norm_act(nc, act, b, s, b.eps5[0:R, :])
            for m in range(H2):
                act.wait_ge(s["mm"], m + 1)
                nc.scalar.activation(halves(b.XT[:, m, :]), b.slot(ring.slot(m))[:, :, 0:HF], ACT.Copy)\
                    .then_inc(s["act"], 1)
            for m in range(H1 + H2):
                j = H2 + m
                act.wait_ge(s["mm"], j + 1)
                buf, mm, col = (b.HT, m, C["b1"] + m) if m < H1 else (b.QT, m - H1, C["b2"] + m - H1)
                if m == H1:
                    act.wait_ge(s["mm"], j + 1)
                nc.scalar.activation(halves(buf[:, mm, :]), b.slot(ring.slot(j))[:, :, 0:HF], ACT.Identity,
                                     bias=b.cols[:, col:col + 1]).then_inc(s["act"], 1)
                if m == H1 - 1 or m == H1 + H2 - 1:
                    n, nm = (1, H1) if m == H1 - 1 else (2, H2)
                    act.wait_ge(s["bn_var"], n)
                    nc.scalar.activation(b.bn_std[:, 0:nm], b.bn_var[:, 0:nm], ACT.Sqrt, bias=b.eps5[:, :])\
                        .then_inc(s["bn_std"], 1)
                    act.wait_ge(s["bn_affine"], n)
                    act.wait_ge(s["act"], j + 1)
                    for q in range(nm):
                        nc.scalar.activation(buf[:, q, :], buf[:, q, :], ACT.Relu, scale=b.bn_scale[:, q:q + 1],
                                             bias=b.bn_bias[:, q:q + 1]).then_inc(s["bn_done"], 1)


def experts_top2(nc, dve, act_unused, c, b, logits, out, s, count):
    v = nc.vector
    for t in range(T):
        c.mark(v.max(b.top_val[0:R, t, :], logits[:, t, :]))
    c.wait()
    for t in range(T):
        c.mark(v.max_index(b.top_idx[0:R, t, :], b.top_val[0:R, t, :], logits[:, t, :]))
    c.wait()
    c.mark(v.tensor_tensor(b.gate_tmp[0:R, :, 0:8], logits, b.top_val[0:R, :, 0:1].to_broadcast([R, T, 8]),
                           ALU.subtract))
    c.link(v.tensor_copy(b.top_idxf[0:R, :, :], b.top_idx[0:R, :, :]))
    for t in range(T):
        c.mark(v.tensor_scalar(b.gate_hot[0:R, t, 0:8], b.iota[0:R, 0:8], b.top_idxf[0:R, t, 0:1], None,
                               ALU.is_equal))
    c.wait()
    for t in range(T):
        c.mark(v.scalar_tensor_tensor(b.gate_hot[0:R, t, 0:8], b.iota[0:R, 0:8], b.top_idxf[0:R, t, 1:2],
                                      b.gate_hot[0:R, t, 0:8], ALU.is_equal, ALU.add))
    c.wait()
    v.memset(b.few[0:R, 0, :], 0.0).then_inc(s["logits_shifted"], 1)
    dve.wait_ge(s["gates_exp"], 1)
    c.link(v.tensor_tensor(b.gate_tmp[0:R, :, 0:8], b.gate_tmp[0:R, :, 0:8], b.gate_hot[0:R, :, 0:8], ALU.mult))
    c.link(v.reduce_sum(b.few[0:R, 1, 0:T], b.gate_tmp[0:R, :, 0:8], AX.X))
    c.link(v.reciprocal(b.few[0:R, 2, 0:T], b.few[0:R, 1, 0:T]))
    v.tensor_tensor(out, b.gate_tmp[0:R, :, 0:8], b.few[0:R, 2, 0:T].unsqueeze(2).to_broadcast([R, T, 8]),
                    ALU.mult).then_inc(s["gates_ready"], 1)


def experts_top2_act(nc, act, b, s):
    act.wait_ge(s["logits_shifted"], 1)
    nc.scalar.activation(b.gate_tmp[0:R, :, 0:8], b.gate_tmp[0:R, :, 0:8], ACT.Exp).then_inc(s["gates_exp"], 1)


def l0_ffn_block(nc, p, b, A):
    s = semaphores(p, "f0", "chain", "loaded", "stats_ready", "std_ready", "xn_ready", "transposed", "xt_ready",
             "logits", "logits_copied", "logits_shifted", "gates_exp", "gates_ready", "gates_t", "gt_ready", "beta_mm", "beta_added",
             "hidden_mm", "hidden_ready", "y_mm", "y_read", "var_ready", "std_e", "affine", "normed", "scaled", "added")
    NE = 8
    W1 = b.W[:, 0:4096].rearrange("p (e k f) -> p e k f", e=NE, k=KD)
    W2 = b.W[:, 4096:8192].rearrange("p (e n) -> p e n", e=NE)
    gamma = b.W[:, 8192:12288].rearrange("p (e n) -> p e n", e=NE)
    b2row = b.W[0:1, 12288:16384].rearrange("p (e n) -> p e n", e=NE)
    S = [b.H[0:R, :, :], b.V[0:R, :, :], b.P[0:R, :, 0:D]]
    C = b.col_of["f0b1"]
    with nc.Block(no_gpsimd_drain=True) as block:
        @block.sync
        def _(sp):
            sp.dma_start(b.router[:, 0:32], A["L0_ffn_router_w"]).then_inc(s["loaded"], 16)
            sp.dma_start(b.RB[0:8, 0:512], A["L0_ffn_beta"]).then_inc(s["loaded"], 16)
            sp.dma_start(b.W[:, 0:4096], A["L0_ffn_w1"]).then_inc(s["loaded"], 16)
            sp.dma_start(b.W[:, 4096:8192], A["L0_ffn_w2"]).then_inc(s["loaded"], 16)
            sp.dma_start(b.W[0:1, 12288:16384], A["L0_ffn_b2"]).then_inc(s["loaded"], 16)
            sp.dma_start(b.W[:, 8192:12288], A["L0_ffn_gamma"].partition_broadcast(128)).then_inc(s["loaded"], 16)

        @block.vector
        def _(dve):
            c = Chain(dve, s["chain"])
            v = nc.vector
            layer_norm_dve(nc, dve, b, c, s, b.X[0:R, :, :], b.XN[0:R, :, :])
            dve.wait_ge(s["logits"], 1)
            v.tensor_copy(b.logits[0:R, :, 0:8], b.ps[0:R, 5, 0:40].rearrange("p (t e) -> p t e", t=T))\
                .then_inc(s["logits_copied"], 1)
            dve.wait_ge(s["logits_copied"], 1)
            experts_top2(nc, dve, None, c, b, b.logits[0:R, :, 0:8], b.gates[0:R, :, 0:8], s, 0)
            for t in range(T):
                dve.wait_ge(s["beta_mm"], t + 1)
                v.tensor_tensor(b.X[0:R, t, :], b.X[0:R, t, :], b.ps[0:R, 4 + t % 2, :], ALU.add)\
                    .then_inc(s["beta_added"], 1)
            dve.wait_ge(s["loaded"], 96)

            def statistics(e):
                sb = S[e % 3]
                for t in range(T):
                    j = e * T + t
                    if e >= 3:
                        dve.wait_ge(s["added"], T * (e - 3) + t + 1)
                    dve.wait_ge(s["y_mm"], j + 1)
                    v.tensor_tensor(sb[:, t, :], b.XN[0:R, t, :], b.ps[0:R, 4 + j % 4, :], ALU.add)\
                        .then_inc(s["y_read"], 1)
                    if e:
                        if t == 0:
                            dve.wait_ge(s["affine"], e)
                    dve.wait_ge(s["y_read"], j + 1)
                    c.mark(v.bn_stats(b.stats[0:R, t, :], sb[:, t, :]))
                c.wait()
                for t in range(T):
                    c.mark(v.bn_aggr(b.mv2[0:R, e % 2, t, :], b.stats[0:R, t, :]))
                c.wait()
                v.tensor_copy(b.var[0:R, 0:T], b.mv2[0:R, e % 2, :, 1]).then_inc(s["var_ready"], 1)

            def affine(e):
                dve.wait_ge(s["std_e"], e + 1)
                sc, bi = b.aff[0:R, e % 2, 0, :], b.aff[0:R, e % 2, 1, :]
                if e >= 2:
                    dve.wait_ge(s["normed"], T * (e - 1))
                c.link(v.reciprocal(sc, b.std[0:R, 0:T]))
                c.link(v.tensor_tensor(sc, sc, b.gates[0:R, :, e], ALU.mult))
                v.scalar_tensor_tensor(bi, b.mv2[0:R, e % 2, :, 0], -1.0, sc, ALU.mult, ALU.mult)\
                    .then_inc(s["affine"], 1)

            def accumulate(e):
                for t in range(T):
                    dve.wait_ge(s["scaled"], e * T + t + 1)
                    if e or t >= 0:
                        dve.wait_ge(s["beta_added"], T)
                    if e:
                        dve.wait_ge(s["added"], T * (e - 1) + t + 1)
                    v.tensor_tensor(b.X[0:R, t, :], b.X[0:R, t, :], S[e % 3][:, t, :], ALU.add)\
                        .then_inc(s["added"], 1)

            statistics(0)
            for e in range(NE):
                affine(e)
                if e + 1 < NE:
                    statistics(e + 1)
                accumulate(e)

        @block.gpsimd
        def _(pool):
            pool.wait_ge(s["loaded"], 96)
            for e in range(NE):
                for t in range(T):
                    pool.wait_ge(s["normed"], e * T + t + 1)
                    nc.gpsimd.tensor_tensor(S[e % 3][:, t, :], S[e % 3][:, t, :], gamma[0:R, e, :], ALU.mult)\
                        .then_inc(s["scaled"], 1)

        @block.tensor
        def _(pe):
            transposes_pe(nc, pe, b, s, b.XN[0:R, :, :], s["xn_ready"])
            pe.wait_ge(s["xt_ready"], T)
            pe.wait_ge(s["loaded"], 96)
            for t in range(T):
                last = matmul_rows(nc, b.ps[0:R, 5, t * 8:(t + 1) * 8], lambda k: b.XT[:, k, t * R:(t + 1) * R],
                                   lambda k: b.router[:, k * 8:(k + 1) * 8], KD)
            last.then_inc(s["logits"], 1)

            def hidden(e):
                if e >= 2:
                    pe.wait_ge(s["hidden_ready"], e - 1)
                matmul_columns(nc, b.slot(e % 2), 128, lambda k: W1[:, e, k, :], lambda k: b.XT[:, k, :], KD)\
                    .then_inc(s["hidden_mm"], 1)

            hidden(0)
            hidden(1)
            pe.wait_ge(s["gates_ready"], 1)
            for t in range(T):
                last = nc.tensor.transpose(b.ps[0:8, 6 + t // 4, (t % 4) * 128:(t % 4) * 128 + R],
                                           b.gates[0:R, t, 0:8], b.ident[0:R, 0:R])
            last.then_inc(s["gates_t"], 1)
            pe.wait_ge(s["gt_ready"], 2)
            pe.wait_ge(s["logits_copied"], 1)
            for t in range(T):
                if t >= 2:
                    pe.wait_ge(s["beta_added"], t - 1)
                nc.tensor.matmul(b.ps[0:R, 4 + t % 2, :], b.GT[0:8, t * R:(t + 1) * R], b.RB[0:8, 0:512],
                                 start=True, stop=True).then_inc(s["beta_mm"], 1)
            pe.wait_ge(s["beta_added"], T)
            for e in range(NE):
                pe.wait_ge(s["hidden_ready"], e + 1)
                for t in range(T):
                    j = e * T + t
                    if j >= 4:
                        pe.wait_ge(s["y_read"], j - 3)
                    bank = b.ps[0:R, 4 + j % 4, :]
                    nc.tensor.matmul(bank, b.ones[0:1, 0:R], b2row[:, e, :], start=True, stop=False)
                    nc.tensor.matmul(bank, b.HT[:, e, t * R:(t + 1) * R], W2[:, e, :], start=False, stop=True)\
                        .then_inc(s["y_mm"], 1)
                if e + 2 < NE:
                    hidden(e + 2)

        @block.scalar
        def _(act):
            layer_norm_act(nc, act, b, s, b.eps5[0:R, :])
            transposes_act(nc, act, b, s, b.XT)
            for e in range(2):
                act.wait_ge(s["hidden_mm"], e + 1)
                nc.scalar.activation(halves(b.HT[:, e, :]), b.slot(e % 2)[:, :, 0:HF], ACT.Relu,
                                     bias=b.cols[:, C + e:C + e + 1]).then_inc(s["hidden_ready"], 1)
            experts_top2_act(nc, act, b, s)
            act.wait_ge(s["gates_t"], 1)
            gt = b.GT[0:8, 0:4 * R].rearrange("p (t n) -> p t n", t=4)
            nc.scalar.activation(gt, b.ps[0:8, 6, :].rearrange("p (t n) -> p t n", t=4)[:, :, 0:R], ACT.Copy)\
                .then_inc(s["gt_ready"], 1)
            nc.scalar.activation(b.GT[0:8, 4 * R:N], b.ps[0:8, 7, 0:R], ACT.Copy).then_inc(s["gt_ready"], 1)
            for e in range(NE):
                act.wait_ge(s["var_ready"], e + 1)
                if e:
                    act.wait_ge(s["affine"], e)
                nc.scalar.activation(b.std[0:R, 0:T], b.var[0:R, 0:T], ACT.Sqrt, bias=b.eps6[0:R, :])\
                    .then_inc(s["std_e"], 1)
                if e + 2 < NE:
                    act.wait_ge(s["hidden_mm"], e + 3)
                    nc.scalar.activation(halves(b.HT[:, e + 2, :]), b.slot(e % 2)[:, :, 0:HF], ACT.Relu,
                                         bias=b.cols[:, C + e + 2:C + e + 3]).then_inc(s["hidden_ready"], 1)
                act.wait_ge(s["affine"], e + 1)
                for t in range(T):
                    nc.scalar.activation(S[e % 3][:, t, :], S[e % 3][:, t, :], ACT.Identity,
                                         scale=b.aff[0:R, e % 2, 0, t:t + 1], bias=b.aff[0:R, e % 2, 1, t:t + 1])\
                        .then_inc(s["normed"], 1)


def l1_gnn_blocks(nc, p, b, A, hb):
    s0 = semaphores(p, "g1s", "chain", "stats_ready", "std_ready", "xn_ready")
    with nc.Block(no_gpsimd_drain=True) as block:
        @block.vector
        def _(dve):
            layer_norm_dve(nc, dve, b, Chain(dve, s0["chain"]), s0, b.X[0:R, :, :], b.H[0:R, :, :])

        @block.scalar
        def _(act):
            layer_norm_act(nc, act, b, s0, b.eps5[0:R, :])

    se = semaphores(p, "g1e", "chain", "slot_begun", "vectors", "weights", "hb_ready", "hb_stored", "idx_copied", "agg_ready", "attr_copied", "edge_mm", "pre_ready", "relu_ready", "hot_ready", "sum_mm", "added")
    sm = semaphores(p, "g1m", "chain", "transposed", "xt_ready", "mm", "act", "dve", "relu", "g_ready",
              "stats_ready", "std_ready", "xn_ready")
    arrived = p.sems("g1_in0", "g1_in1", "g1_in2", "g1_in3")
    U, turns = SLOT_UNROLL, NSLOT // SLOT_UNROLL
    w0 = NSLOT * 128
    We = b.W[:, w0:w0 + 512]
    W1 = b.W[:, w0 + 512:w0 + 2560].rearrange("p (k n) -> p k n", k=KD)
    W2 = b.W[:, w0 + 2560:w0 + 4608].rearrange("p (k n) -> p k n", k=KD)
    AGG = b.XN
    agg_flat = b.XN[:, :, :].rearrange("p t d -> p (t d)")
    with nc.Fori(0, 3) as layer:
        with nc.Block() as block:
            @block.sync
            def _(sp):
                for x in sm.values():
                    sp.sem_clear(x)
                sp.dma_start(b.RB[:, 0:2048], A["L1_gnn_rows"][bass.ds(layer, 1), :].rearrange("a n -> (a n)")
                             .partition_broadcast(128)).then_inc(se["vectors"], 16)
                sp.dma_start(b.eps_col[:, :], A["L1_gnn_eps"][bass.ds(layer, 1)].partition_broadcast(128))\
                    .then_inc(se["vectors"], 16)
                sp.dma_start(b.W[:, w0:w0 + 512], A["L1_gnn_We"][bass.ds(layer, 1), :, :]
                             .rearrange("a p n -> p (a n)")).then_inc(se["weights"], 16)
                sp.dma_start(b.W[:, w0 + 512:w0 + 4608], A["L1_gnn_W12"][bass.ds(layer, 1), :, :]
                             .rearrange("a p n -> p (a n)")).then_inc(se["weights"], 16)
                sp.dma_start(b.lcols[:, 0:4], A["L1_gnn_b1"][bass.ds(layer, 1), :, :]
                             .rearrange("a p n -> p (a n)")).then_inc(se["weights"], 16)
                for t in range(T):
                    sp.wait_ge(se["hb_ready"], t + 1)
                    sp.dma_start(hb[t * R:(t + 1) * R, :], b.V[0:R, t, :]).then_inc(se["hb_stored"], 16)
                sp.wait_ge(se["weights"], 48)

            @block.gpsimd
            def _(pool):
                pool.wait_ge(se["hb_stored"], 16 * T)

                def turn(i, first):
                    for u in range(U):
                        t = i * U + u
                        if not first:
                            pool.wait_ge(arrived[u], 16 * (layer * turns + i))
                        nc.gpsimd.tensor_copy(b.gather_idx[u][:, :], b.slot_src[:, bass.ds(t, 1)])\
                            .then_inc(se["idx_copied"], 1)
                        pool.wait_ge(se["idx_copied"], t + 1)
                        if not first:
                            pool.wait_ge(se["pre_ready"], t - U + 1)
                        pool.sem_inc(se["slot_begun"], 1)
                        nc.gpsimd.indirect_dma_start(
                            b.gathered[u][:, :], None, hb,
                            bass.IndirectOffsetOnAxis(ap=b.gather_idx[u][:, 0:1], axis=0)).then_inc(arrived[u], 16)

                turn(0, True)
                with pool.Fori(1, turns) as i:
                    turn(i, False)

            @block.tensor
            def _(pe):
                pe.wait_ge(se["weights"], 48)

                def edge_product(t, u):
                    pe.wait_ge(se["attr_copied"], t + 1)
                    wait_positive(pe, se["pre_ready"], t - 1)
                    nc.tensor.matmul(b.ps[:, u % 2, :], b.attr[u % U][:, :], We, start=True, stop=True)\
                        .then_inc(se["edge_mm"], 1)

                def turn(i, last):
                    for u in range(U):
                        t = i * U + u
                        if not (last and u == U - 1):
                            edge_product(t + 1, u + 1)
                        pe.wait_ge(se["hot_ready"], t + 1)
                        pe.wait_ge(se["relu_ready"], t + 1)
                        wait_positive(pe, se["added"], t - 1)
                        nc.tensor.matmul(b.ps[0:R, 2 + u % 2, :], b.hot[u][:, :], b.message[u][:, :],
                                         start=True, stop=True).then_inc(se["sum_mm"], 1)

                edge_product(0, 0)
                turn(0, False)
                with pe.Fori(1, turns - 1) as i:
                    turn(i, False)
                turn(turns - 1, True)

            @block.scalar
            def _(act):
                def turn(i):
                    for u in range(U):
                        t = i * U + u
                        act.wait_ge(se["pre_ready"], t + 1)
                        nc.scalar.activation(b.message[u][:, :], b.message[u][:, :], ACT.Relu)\
                            .then_inc(se["relu_ready"], 1)

                turn(0)
                with act.Fori(1, turns) as i:
                    turn(i)

            @block.vector
            def _(dve):
                v = nc.vector
                c = Chain(dve, se["chain"])
                dve.wait_ge(se["vectors"], 32)
                for t in range(T):
                    v.tensor_tensor(b.V[0:R, t, :], b.H[0:R, t, :], b.RB[0:R, 0:512], ALU.add)\
                        .then_inc(se["hb_ready"], 1)
                c.link(v.tensor_scalar(b.eps_col[:, :], b.eps_col[:, :], 1.0, None, ALU.add))
                for t in range(T):
                    v.tensor_scalar(AGG[0:R, t, :], b.H[0:R, t, :], b.eps_col[0:R, 0:1], None, ALU.mult)\
                        .then_inc(se["agg_ready"], 1)

                def copy_attributes(t, u):
                    wait_positive(dve, se["edge_mm"], t - U + 1)
                    v.tensor_scalar(b.attr[u % U][:, :], b.EAT[:, bass.ds(t * 128, 128)], 1.0, None, ALU.mult)\
                        .then_inc(se["attr_copied"], 1)

                def add_sum(t, u):
                    off = dve.value_load(b.slot_off[0:1, bass.ds(t, 1)], min_val=0, max_val=(T - 1) * D)
                    dve.wait_ge(se["sum_mm"], t + 1)
                    wait_positive(dve, se["added"], t)
                    v.tensor_tensor(agg_flat[0:R, bass.ds(off, D)], agg_flat[0:R, bass.ds(off, D)],
                                    b.ps[0:R, 2 + u % 2, :], ALU.add).then_inc(se["added"], 1)

                def turn(i, first, last):
                    for u in range(U):
                        t = i * U + u
                        if not (last and u >= U - 2):
                            copy_attributes(t + 2, u + 2)
                        if not first:
                            dve.wait_ge(se["sum_mm"], t - U + 1)
                        dve.wait_ge(arrived[u], 16 * (layer * turns + i + 1))
                        dve.wait_ge(se["edge_mm"], t + 1)
                        v.tensor_tensor(b.message[u][:, :], b.gathered[u][:, :], b.ps[:, u % 2, :], ALU.add)\
                            .then_inc(se["pre_ready"], 1)
                        v.tensor_scalar(b.hot[u][:, :], b.iota[:, 0:R], b.slot_dst[:, bass.ds(t, 1)], None,
                                        ALU.is_equal).then_inc(se["hot_ready"], 1)
                        if not (first and u == 0):
                            add_sum(t - 1, u + 1)

                dve.wait_ge(se["agg_ready"], T)
                copy_attributes(0, 0)
                copy_attributes(1, 1)
                turn(0, True, False)
                with dve.Fori(1, turns - 1) as i:
                    turn(i, False, False)
                turn(turns - 1, False, True)
                add_sum(NSLOT - 1, U - 1)

        s = sm
        ring = Ring(["act"] * 4 + ["dve"] * 5, {"act": s["act"], "dve": s["dve"]}, 3)
        with nc.Block(no_gpsimd_drain=True) as block:
            @block.sync
            def _(sp):
                for x in se.values():
                    sp.sem_clear(x)

            @block.tensor
            def _(pe):
                transposes_pe(nc, pe, b, s, AGG[0:R, :, :], None)
                pe.wait_ge(s["xt_ready"], T)
                for m in range(KD):
                    ring.acquire(pe, m)
                    matmul_columns(nc, b.slot(ring.slot(m)), 128, lambda k: W1[:, k, m * 128:(m + 1) * 128],
                                   lambda k: b.XT[:, k, :], KD).then_inc(s["mm"], 1)
                ring.wait_read(pe, KD - 1)
                for t in range(T):
                    ring.acquire(pe, KD + t)
                    matmul_rows(nc, b.slot(ring.slot(KD + t))[0:R, 0, :], lambda k: b.HT[:, k, t * R:(t + 1) * R],
                                lambda k: W2[:, k, :], KD).then_inc(s["mm"], 1)

            @block.scalar
            def _(act):
                transposes_act(nc, act, b, s, b.XT)
                for m in range(KD):
                    act.wait_ge(s["mm"], m + 1)
                    nc.scalar.activation(halves(b.HT[:, m, :]), b.slot(ring.slot(m))[:, :, 0:HF], ACT.Relu,
                                         bias=b.lcols[:, m:m + 1]).then_inc(s["act"], 1)
                for t in range(T):
                    act.wait_ge(s["dve"], t + 1)
                    nc.scalar.activation(b.V[0:R, t, :], b.V[0:R, t, :], ACT.Relu).then_inc(s["g_ready"], 1)
                layer_norm_act(nc, act, b, s, b.eps5[0:R, :])

            @block.vector
            def _(dve):
                v = nc.vector
                c = Chain(dve, s["chain"])
                for t in range(T):
                    j = KD + t
                    dve.wait_ge(s["mm"], j + 1)
                    v.tensor_tensor(b.V[0:R, t, :], b.RB[0:R, 512:1024], b.slot(ring.slot(j))[0:R, 0, :], ALU.add)\
                        .then_inc(s["dve"], 1)
                dve.wait_ge(s["g_ready"], T)
                layer_norm_dve(nc, dve, b, c, s, b.V[0:R, :, :], b.H[0:R, :, :])
                dve.wait_ge(s["xn_ready"], T)
                for t in range(T):
                    c.mark(v.tensor_tensor(b.H[0:R, t, :], b.H[0:R, t, :], b.RB[0:R, 1024:1536], ALU.mult))
                c.wait()
                for t in range(T):
                    c.mark(v.tensor_tensor(b.H[0:R, t, :], b.H[0:R, t, :], b.RB[0:R, 1536:2048], ALU.add))

    s = semaphores(p, "g1f", "loaded", "transposed", "xt_ready", "mm", "sum", "dve")
    Wf = b.W[:, 0:2048].rearrange("p (k n) -> p k n", k=KD)
    with nc.Block(no_gpsimd_drain=True) as block:
        @block.sync
        def _(sp):
            sp.dma_start(b.W[:, 0:2048], A["L1_gnn_Wf"]).then_inc(s["loaded"], 16)
            sp.dma_start(b.RB[:, 0:512], A["L1_gnn_bf"].partition_broadcast(128)).then_inc(s["loaded"], 16)

        @block.tensor
        def _(pe):
            transposes_pe(nc, pe, b, s, b.H[0:R, :, :], None)
            pe.wait_ge(s["xt_ready"], T)
            pe.wait_ge(s["loaded"], 32)
            for t in range(T):
                matmul_rows(nc, b.ps[0:R, t, :], lambda k: b.XT[:, k, t * R:(t + 1) * R], lambda k: Wf[:, k, :], KD)\
                    .then_inc(s["mm"], 1)

        @block.scalar
        def _(act):
            transposes_act(nc, act, b, s, b.XT)

        @block.vector
        def _(dve):
            dve.wait_ge(s["loaded"], 32)
            for t in range(T):
                nc.vector.tensor_tensor(b.X[0:R, t, :], b.X[0:R, t, :], b.RB[0:R, 0:512], ALU.add)\
                    .then_inc(s["sum"], 1)
            dve.wait_ge(s["sum"], T)
            for t in range(T):
                dve.wait_ge(s["mm"], t + 1)
                nc.vector.tensor_tensor(b.X[0:R, t, :], b.X[0:R, t, :], b.ps[0:R, t, :], ALU.add).then_inc(s["dve"], 1)


def l1_ffn_blocks(nc, p, b, A):
    NE = 6
    s = semaphores(p, "f1", "chain", "loaded", "stats_ready", "std_ready", "xn_ready", "transposed", "xt_ready",
             "logits", "shifted", "exp_ready")
    W1 = b.W[:, 0:3072].rearrange("p (e k f) -> p e k f", e=NE, k=KD)
    W2 = b.W[:, 3072:6144].rearrange("p (e n) -> p e n", e=NE)
    with nc.Block(no_gpsimd_drain=True) as block:
        @block.sync
        def _(sp):
            sp.dma_start(b.router[:, 0:KD * NE], A["L1_ffn_w_gating"]).then_inc(s["loaded"], 16)
            sp.dma_start(b.RB[:, 0:512], A["L1_ffn_gamma"].partition_broadcast(128)).then_inc(s["loaded"], 16)
            sp.dma_start(b.W[:, 0:3072], A["L1_ffn_w1"]).then_inc(s["loaded"], 16)
            sp.dma_start(b.W[:, 3072:6144], A["L1_ffn_w2"]).then_inc(s["loaded"], 16)
            sp.wait_ge(s["loaded"], 64)

        @block.vector
        def _(dve):
            c = Chain(dve, s["chain"])
            v = nc.vector
            c.mark(v.memset(b.logits[0:R, :, 0:8], -HUGE))
            layer_norm_dve(nc, dve, b, c, s, b.X[0:R, :, :], b.XN[0:R, :, :])
            dve.wait_ge(s["logits"], 1)
            c.link(v.tensor_copy(b.logits[0:R, :, 0:NE], b.ps[0:R, 5, 0:T * NE].rearrange("p (t e) -> p t e", t=T)))
            for t in range(T):
                c.mark(v.max(b.top_val[0:R, t, :], b.logits[0:R, t, 0:8]))
            c.wait()
            for t in range(T):
                c.mark(v.max_index(b.top_idx[0:R, t, :], b.top_val[0:R, t, :], b.logits[0:R, t, 0:8]))
            c.wait()
            c.mark(v.tensor_copy(b.top_idxf[0:R, :, :], b.top_idx[0:R, :, :]))
            v.tensor_tensor(b.gate_tmp[0:R, :, 0:NE], b.logits[0:R, :, 0:NE],
                            b.top_val[0:R, :, 0:1].to_broadcast([R, T, NE]), ALU.subtract).then_inc(s["shifted"], 1)
            c.wait()
            for t in range(T):
                c.mark(v.tensor_scalar(b.gate_hot[0:R, t, 0:NE], b.iota[0:R, 0:NE], b.top_idxf[0:R, t, 0:1], None,
                                       ALU.is_equal))
            dve.wait_ge(s["exp_ready"], 1)
            few = b.few[0:R]
            wide = [R, T, NE]
            c.link(v.reduce_sum(few[:, 0, 0:T], b.gate_tmp[0:R, :, 0:NE], AX.X))
            c.link(v.reciprocal(few[:, 1, 0:T], few[:, 0, 0:T]))
            c.link(v.tensor_tensor(b.gate_tmp[0:R, :, 0:NE], b.gate_tmp[0:R, :, 0:NE],
                                   few[:, 1, 0:T].unsqueeze(2).to_broadcast(wide), ALU.mult))
            c.link(v.reduce_max(few[:, 2, 0:T], b.gate_tmp[0:R, :, 0:NE], AX.X))
            c.link(v.tensor_tensor(b.logits[0:R, :, 0:NE], b.gate_tmp[0:R, :, 0:NE], b.gate_hot[0:R, :, 0:NE],
                                   ALU.mult))
            c.link(v.tensor_tensor(b.gate_tmp[0:R, :, 0:NE], b.gate_tmp[0:R, :, 0:NE], b.logits[0:R, :, 0:NE],
                                   ALU.subtract))
            c.link(v.reduce_max(few[:, 3, 0:T], b.gate_tmp[0:R, :, 0:NE], AX.X))
            c.link(v.tensor_tensor(few[:, 3, 0:T], few[:, 2, 0:T], few[:, 3, 0:T], ALU.add))
            c.link(v.tensor_scalar(few[:, 3, 0:T], few[:, 3, 0:T], 1e-9, None, ALU.add))
            c.link(v.reciprocal(few[:, 4, 0:T], few[:, 3, 0:T]))
            c.link(v.tensor_tensor(few[:, 4, 0:T], few[:, 4, 0:T], few[:, 2, 0:T], ALU.mult))
            c.link(v.tensor_tensor(b.gates[0:R, :, 0:NE], b.gate_hot[0:R, :, 0:NE],
                                   few[:, 4, 0:T].unsqueeze(2).to_broadcast(wide), ALU.mult))

        @block.tensor
        def _(pe):
            transposes_pe(nc, pe, b, s, b.XN[0:R, :, :], s["xn_ready"])
            pe.wait_ge(s["xt_ready"], T)
            pe.wait_ge(s["loaded"], 64)
            for t in range(T):
                last = matmul_rows(nc, b.ps[0:R, 5, t * NE:(t + 1) * NE], lambda k: b.XT[:, k, t * R:(t + 1) * R],
                                   lambda k: b.router[:, k * NE:(k + 1) * NE], KD)
            last.then_inc(s["logits"], 1)

        @block.scalar
        def _(act):
            layer_norm_act(nc, act, b, s, b.eps5[0:R, :])
            transposes_act(nc, act, b, s, b.XT)
            act.wait_ge(s["shifted"], 1)
            nc.scalar.activation(b.gate_tmp[0:R, :, 0:NE], b.gate_tmp[0:R, :, 0:NE], ACT.Exp)\
                .then_inc(s["exp_ready"], 1)

    s = semaphores(p, "f1x", "chain", "stats_ready", "std_ready", "xn_ready", "scaled", "transposed", "xt_ready", "hidden_mm",
             "hidden_ready", "y_mm", "added")
    with nc.Block(no_gpsimd_drain=True) as block:
        @block.vector
        def _(dve):
            c = Chain(dve, s["chain"])
            v = nc.vector
            layer_norm_dve(nc, dve, b, c, s, b.XN[0:R, :, :], b.H[0:R, :, :])
            for t in range(T):
                dve.wait_ge(s["xn_ready"], t + 1)
                v.tensor_tensor(b.H[0:R, t, :], b.H[0:R, t, :], b.RB[0:R, 0:512], ALU.mult).then_inc(s["scaled"], 1)
            for j in range(NE * T):
                e, t = j // T, j % T
                dve.wait_ge(s["y_mm"], j + 1)
                if e:
                    dve.wait_ge(s["added"], j - T + 1)
                v.scalar_tensor_tensor(b.X[0:R, t, :], b.ps[0:R, 4 + j % 4, :], b.gates[0:R, t, e:e + 1],
                                       b.X[0:R, t, :], ALU.mult, ALU.add).then_inc(s["added"], 1)

        @block.tensor
        def _(pe):
            transposes_pe(nc, pe, b, s, b.H[0:R, :, :], s["scaled"])
            pe.wait_ge(s["xt_ready"], T)

            def hidden(e):
                if e >= 2:
                    pe.wait_ge(s["hidden_ready"], e - 1)
                matmul_columns(nc, b.slot(e % 2), 128, lambda k: W1[:, e, k, :], lambda k: b.XT[:, k, :], KD)\
                    .then_inc(s["hidden_mm"], 1)

            hidden(0)
            for e in range(NE):
                if e + 1 < NE:
                    hidden(e + 1)
                pe.wait_ge(s["hidden_ready"], e + 1)
                for t in range(T):
                    j = e * T + t
                    if j >= 4:
                        pe.wait_ge(s["added"], j - 3)
                    nc.tensor.matmul(b.ps[0:R, 4 + j % 4, :], b.HT[:, e, t * R:(t + 1) * R], W2[:, e, :],
                                     start=True, stop=True).then_inc(s["y_mm"], 1)

        @block.scalar
        def _(act):
            layer_norm_act(nc, act, b, s, b.eps5[0:R, :])
            transposes_act(nc, act, b, s, b.XT)
            for e in range(NE):
                act.wait_ge(s["hidden_mm"], e + 1)
                nc.scalar.activation(halves(b.HT[:, e, :]), b.slot(e % 2)[:, :, 0:HF], ACT.Gelu)\
                    .then_inc(s["hidden_ready"], 1)


def l2_start_block(nc, p, b, A):
    s = semaphores(p, "g2s", "chain", "stats_ready", "std_ready", "xn_ready", "loaded", "angles", "embedded", "h1_mm", "h1",
             "cond_mm", "cond", "cnt_max", "log_ready", "masked", "ones")
    NF = 64
    ph, q, r, emb = (b.XT[0:NF, i, :] for i in range(4))
    hid = b.QT[0:16, 0, :]
    C = b.col_of
    c1, c2 = 6.28125, 0.0019340515136718750
    c3 = TWO_PI - c1 - c2
    magic = 12582912.0
    with nc.Block(no_gpsimd_drain=True) as block:
        @block.sync
        def _(sp):
            sp.dma_start(b.XT[0:NF, 0, 0:N], A["node_vec1"].partition_broadcast(NF)).then_inc(s["loaded"], 16)
            sp.dma_start(b.router[0:NF, 0:16], A["L2_gnn_f_w1"]).then_inc(s["loaded"], 16)
            sp.dma_start(b.router[0:16, 16:32], A["L2_gnn_f_w2"]).then_inc(s["loaded"], 16)

        @block.gpsimd
        def _(pool):
            nc.gpsimd.memset(b.GT[0:32, :], 1.0).then_inc(s["ones"], 1)

        @block.vector
        def _(dve):
            c = Chain(dve, s["chain"])
            v = nc.vector
            for t in range(T):
                c.mark(v.tensor_scalar(b.P[0:R, t, :], b.CNT[0:R, t, :], 1.0, None, ALU.max))
                c.mark(v.reduce_max(b.row_has[0:R, t:t + 1], b.CNT[0:R, t, :], AX.X))
            c.wait()
            v.tensor_scalar(b.row_has[0:R, :], b.row_has[0:R, :], 1.0, None, ALU.min).then_inc(s["cnt_max"], 1)
            dve.wait_ge(s["loaded"], 48)
            c.link(v.tensor_scalar(ph, ph, b.cols[0:NF, C["freq"]:C["freq"] + 1], None, ALU.mult))
            c.link(v.tensor_scalar(q, ph, 1.0 / TWO_PI, None, ALU.mult))
            c.link(v.tensor_scalar(q, q, magic, None, ALU.add))
            c.link(v.tensor_scalar(q, q, magic, None, ALU.subtract))
            c.link(v.scalar_tensor_tensor(r, q, -c1, ph, ALU.mult, ALU.add))
            c.link(v.scalar_tensor_tensor(r, q, -c2, r, ALU.mult, ALU.add))
            c.link(v.scalar_tensor_tensor(r, q, -c3, r, ALU.mult, ALU.add))
            c.link(v.tensor_scalar(r, r, 3.1415925, -3.1415925, ALU.min, ALU.max))
            c.link(v.tensor_scalar(q[32:64], r[32:64], -1.0, None, ALU.mult))
            v.tensor_tensor(r[32:64], r[32:64], q[32:64], ALU.max).then_inc(s["angles"], 1)
            layer_norm_dve(nc, dve, b, c, s, b.X[0:R, :, :], b.H[0:R, :, :])
            dve.wait_ge(s["log_ready"], 1)
            c.mark(v.tensor_scalar(b.P[0:R, :, :], b.CNT[0:R, :, :], 1.0, 1.0, ALU.min, ALU.subtract))
            c.wait()
            v.scalar_tensor_tensor(b.LOGC[0:R, :, :], b.P[0:R, :, :], HUGE, b.LOGC[0:R, :, :], ALU.mult, ALU.add)\
                .then_inc(s["masked"], 1)

        @block.tensor
        def _(pe):
            pe.wait_ge(s["loaded"], 48)
            pe.wait_ge(s["embedded"], 2)
            matmul_columns(nc, b.slot(0), 16, lambda k: b.router[0:NF, 0:16], lambda k: emb, 1).then_inc(s["h1_mm"], 1)
            pe.wait_ge(s["h1"], 1)
            matmul_columns(nc, b.slot(1), 16, lambda k: b.router[0:16, 16:32], lambda k: hid, 1).then_inc(s["cond_mm"], 1)

        @block.scalar
        def _(act):
            act.wait_ge(s["cnt_max"], 1)
            nc.scalar.activation(b.LOGC[0:R, :, :], b.P[0:R, :, :], ACT.Ln).then_inc(s["log_ready"], 1)
            act.wait_ge(s["angles"], 1)
            nc.scalar.activation(emb[0:32], r[0:32], ACT.Sin).then_inc(s["embedded"], 1)
            nc.scalar.activation(emb[32:64], r[32:64], ACT.Sin, scale=-1.0, bias=b.half_pi[32:64, :])\
                .then_inc(s["embedded"], 1)
            layer_norm_act(nc, act, b, s, b.eps5[0:R, :])
            act.wait_ge(s["h1_mm"], 1)
            nc.scalar.activation(halves(hid), b.slot(0)[0:16, :, 0:HF], ACT.Silu,
                                 bias=b.cols[0:16, C["f_b1"]:C["f_b1"] + 1]).then_inc(s["h1"], 1)
            act.wait_ge(s["cond_mm"], 1)
            act.wait_ge(s["ones"], 1)
            nc.scalar.activation(halves(b.GT[0:16, :]), b.slot(1)[0:16, :, 0:HF], ACT.Identity,
                                 bias=b.cols[0:16, C["f_b2"]:C["f_b2"] + 1]).then_inc(s["cond"], 1)


def conditioned_norm_dve(nc, dve, b, c, s):
    v = nc.vector
    layer_norm_dve(nc, dve, b, c, s, b.H[0:R, :, :], b.XN[0:R, :, :])
    for t in range(T):
        z = b.XN[0:R, t, :]
        dve.wait_ge(s["xn_ready"], t + 1)
        dve.wait_ge(s["cond_mm"], t + 1)
        c.link(v.scalar_tensor_tensor(z, b.ps[0:R, 2 * (t % 2), :], 1.0, z, ALU.add, ALU.mult))
        v.tensor_tensor(z, z, b.ps[0:R, 2 * (t % 2) + 1, :], ALU.add).then_inc(s["y_ready"], 1)


def conditioned_norm_pe(nc, pe, b, s, affine):
    for t in range(T):
        if t >= 2:
            pe.wait_ge(s["y_ready"], t - 1)
        for a in range(2):
            last = nc.tensor.matmul(b.ps[0:R, 2 * (t % 2) + a, :], b.GT[0:17, t * R:(t + 1) * R],
                                    affine[:, a * D:(a + 1) * D], start=True, stop=True)
        last.then_inc(s["cond_mm"], 1)
    transposes_pe(nc, pe, b, s, b.XN[0:R, :, :], s["y_ready"])
    pe.wait_ge(s["xt_ready"], T)


def l2_gnn_blocks(nc, p, b, A):
    norm = ("chain", "loaded", "stats_ready", "std_ready", "xn_ready", "cond_mm", "y_ready", "transposed", "xt_ready")
    sq = semaphores(p, "g2q", *norm, "vectors", "mm", "act", "dve")
    sa = semaphores(p, "g2a", "chain", "score_mm", "score_read", "shift_ready", "exp_ready", "p_ready", "t_mm", "pt_ready", "ot_mm",
              "ot_ready", "out_mm", "out_read", "added", "pad_zero")
    sm = semaphores(p, "g2m", *norm, "mm", "act", "dve", "added")
    weights_o, weights_m = p.sems("g2_wo_loaded", "g2_wm_loaded")
    Wqkv = [b.W[:, 2048 * i:2048 * (i + 1)].rearrange("p (k n) -> p k n", k=KD) for i in range(3)]
    Wo = b.W[:, 6144:8192].rearrange("p (k n) -> p k n", k=KD)
    M1 = b.W[:, 8192:10240].rearrange("p (k n) -> p k n", k=KD)
    M2 = b.W[:, 10240:12288].rearrange("p (k n) -> p k n", k=KD)
    P = [b.P[0:R, :, :], b.W[0:R, 12288:12288 + T * NP].rearrange("p (t n) -> p t n", t=T)]
    NH = 4
    scale = 128.0 ** -0.5
    with nc.Fori(0, 4) as layer:
        def part(name):
            return A[name][bass.ds(layer, 1), :, :].rearrange("a p n -> p (a n)")

        s = sq
        ring = Ring(["dve"] * 4 + ["act"] * 4 + ["dve"] * 5, {"act": s["act"], "dve": s["dve"]}, 3)
        with nc.Block(no_gpsimd_drain=True) as block:
            @block.sync
            def _(sp):
                for x in [*sm.values(), weights_m]:
                    sp.sem_clear(x)
                for i in range(2):
                    sp.dma_start(b.affine[i], part("L2_gnn_sb")[:, 1024 * i:1024 * (i + 1)]).then_inc(s["vectors"], 16)
                sp.dma_start(b.W[:, 0:6144], part("L2_gnn_Wqkv")).then_inc(s["loaded"], 16)
                sp.dma_start(b.lcols[:, 0:12], part("L2_gnn_cols")).then_inc(s["loaded"], 16)
                sp.dma_start(b.RB[:, 0:1536], A["L2_gnn_rows"][bass.ds(layer, 1), :].rearrange("a n -> (a n)")
                             .partition_broadcast(128)).then_inc(s["loaded"], 16)
                sp.dma_start(b.W[:, 6144:8192], part("L2_gnn_wo")).then_inc(weights_o, 16)
                sp.dma_start(b.W[:, 8192:12288], part("L2_gnn_Wm")).then_inc(weights_m, 16)

            @block.vector
            def _(dve):
                c = Chain(dve, s["chain"])
                v = nc.vector
                conditioned_norm_dve(nc, dve, b, c, s)
                dve.wait_ge(s["loaded"], 48)
                for m in range(NH):
                    dve.wait_ge(s["mm"], m + 1)
                    v.tensor_scalar(halves(b.QT[:, m, :]), b.slot(ring.slot(m))[:, :, 0:HF], b.lcols[:, m:m + 1],
                                    scale, ALU.add, ALU.mult).then_inc(s["dve"], 1)
                for t in range(T):
                    j = 2 * NH + t
                    dve.wait_ge(s["mm"], j + 1)
                    v.tensor_tensor(b.V[0:R, t, :], b.slot(ring.slot(j))[0:R, 0, :], b.RB[0:R, 0:D], ALU.add)\
                        .then_inc(s["dve"], 1)

            @block.tensor
            def _(pe):
                pe.wait_ge(s["vectors"], 32)
                conditioned_norm_pe(nc, pe, b, s, b.affine[0])
                pe.wait_ge(s["loaded"], 48)
                for j in range(2 * NH):
                    ring.acquire(pe, j)
                    m = j % NH
                    matmul_columns(nc, b.slot(ring.slot(j)), 128,
                                   lambda k: Wqkv[j // NH][:, k, m * 128:(m + 1) * 128],
                                   lambda k: b.XT[:, k, :], KD).then_inc(s["mm"], 1)
                for t in range(T):
                    j = 2 * NH + t
                    ring.acquire(pe, j)
                    matmul_rows(nc, b.slot(ring.slot(j))[0:R, 0, :], lambda k: b.XT[:, k, t * R:(t + 1) * R],
                                lambda k: Wqkv[2][:, k, :], KD).then_inc(s["mm"], 1)

            @block.scalar
            def _(act):
                layer_norm_act(nc, act, b, s, b.eps5[0:R, :])
                transposes_act(nc, act, b, s, b.XT)
                act.wait_ge(s["loaded"], 48)
                for m in range(NH):
                    j = NH + m
                    act.wait_ge(s["mm"], j + 1)
                    nc.scalar.activation(halves(b.KT[:, m, :]), b.slot(ring.slot(j))[:, :, 0:HF], ACT.Identity,
                                         bias=b.lcols[:, 4 + m:5 + m]).then_inc(s["act"], 1)

        s = sa
        with nc.Block(no_gpsimd_drain=True) as block:
            @block.sync
            def _(sp):
                for x in sq.values():
                    sp.sem_clear(x)

            @block.gpsimd
            def _(pool):
                nc.gpsimd.memset(b.PT[:, :, N:NP], 0.0).then_inc(s["pad_zero"], 1)

            @block.tensor
            def _(pe):
                def score(h, t):
                    j = h * T + t
                    if j >= 2:
                        pe.wait_ge(s["score_read"], j - 1)
                    matmul_columns(nc, b.slot(j % 2), R, lambda k: b.QT[:, h, t * R:(t + 1) * R],
                                   lambda k: b.KT[:, h, :], 1).then_inc(s["score_mm"], 1)

                for t in range(T):
                    score(0, t)
                for h in range(NH):
                    for t in range(T):
                        if h + 1 < NH:
                            score(h + 1, t)
                        j = h * T + t
                        pe.wait_ge(s["p_ready"], j + 1)
                        if j:
                            pe.wait_ge(s["pt_ready"], 2 * j)
                        for d in range(T):
                            last = nc.tensor.transpose(b.ps[0:R, 4 + d // 4, (d % 4) * 128:(d % 4) * 128 + R],
                                                       P[h % 2][:, t, d * R:(d + 1) * R], b.ident[0:R, 0:R])
                        last.then_inc(s["t_mm"], 1)
                    pe.wait_ge(s["pt_ready"], 2 * T * (h + 1))
                    pe.wait_ge(s["pad_zero"], 1)
                    if h:
                        pe.wait_ge(s["ot_ready"], h)
                    matmul_columns(nc, b.slot(3), 128, lambda k: b.V[0:R, k, h * 128:(h + 1) * 128],
                                   lambda k: b.PT[0:R, k, :], T).then_inc(s["ot_mm"], 1)
                pe.wait_ge(s["ot_ready"], NH)
                pe.wait_ge(weights_o, 16)
                for t in range(T):
                    if t >= 4:
                        pe.wait_ge(s["out_read"], t - 3)
                    matmul_rows(nc, b.ps[0:R, t % 4, :], lambda k: b.XT[:, k, t * R:(t + 1) * R],
                                lambda k: Wo[:, k, :], KD).then_inc(s["out_mm"], 1)

            @block.vector
            def _(dve):
                c = Chain(dve, s["chain"])
                v = nc.vector

                def normalise(j):
                    h, t = j // T, j % T
                    dve.wait_ge(s["exp_ready"], j + 1)
                    c.link(v.reciprocal(b.den[0:R, j:j + 1], b.den[0:R, j:j + 1]))
                    v.tensor_scalar(P[h % 2][:, t, :], P[h % 2][:, t, :], b.den[0:R, j:j + 1],
                                    b.row_has[0:R, t:t + 1], ALU.mult, ALU.mult).then_inc(s["p_ready"], 1)

                for j in range(NH * T):
                    h, t = j // T, j % T
                    dve.wait_ge(s["score_mm"], j + 1)
                    if h >= 2:
                        dve.wait_ge(s["t_mm"], (h - 2) * T + t + 1)
                    nc.vector.tensor_tensor_reduce(
                        out=halves(P[h % 2][:, t, :]), in0=b.slot(j % 2)[0:R, :, 0:HF], in1=halves(b.LOGC[0:R, t, :]),
                        scale=1.0, scalar=-3e38, op0=ALU.add, op1=ALU.max,
                        accum_out=b.smax[0:R, j:j + 1]).then_inc(s["score_read"], 1)
                    dve.wait_ge(s["score_read"], j + 1)
                    v.tensor_scalar(b.nmax[0:R, j:j + 1], b.smax[0:R, j:j + 1], -1.0, None, ALU.mult)\
                        .then_inc(s["shift_ready"], 1)
                    if j:
                        normalise(j - 1)
                normalise(NH * T - 1)
                for t in range(T):
                    dve.wait_ge(s["out_mm"], t + 1)
                    v.tensor_tensor(b.XN[0:R, t, :], b.RB[0:R, D:2 * D], b.ps[0:R, t % 4, :], ALU.add)\
                        .then_inc(s["out_read"], 1)
                    dve.wait_ge(s["out_read"], t + 1)
                    v.tensor_tensor(b.H[0:R, t, :], b.H[0:R, t, :], b.XN[0:R, t, :], ALU.add).then_inc(s["added"], 1)

            @block.scalar
            def _(act):
                def exponential(j):
                    h, t = j // T, j % T
                    act.wait_ge(s["shift_ready"], j + 1)
                    nc.scalar.activation(P[h % 2][:, t, :], P[h % 2][:, t, :], ACT.Exp, bias=b.nmax[0:R, j:j + 1],
                                         accum_out=b.den[0:R, j:j + 1]).then_inc(s["exp_ready"], 1)

                for t in range(T):
                    exponential(t)
                for h in range(NH):
                    for t in range(T):
                        if h + 1 < NH:
                            exponential((h + 1) * T + t)
                        act.wait_ge(s["t_mm"], h * T + t + 1)
                        if h:
                            act.wait_ge(s["ot_mm"], h)
                        nc.scalar.activation(b.PT[0:R, 0:4, t * R:(t + 1) * R],
                                             b.ps[0:R, 4, :].rearrange("p (d n) -> p d n", d=4)[:, :, 0:R],
                                             ACT.Copy).then_inc(s["pt_ready"], 1)
                        nc.scalar.activation(b.PT[0:R, 4, t * R:(t + 1) * R], b.ps[0:R, 5, 0:R], ACT.Copy)\
                            .then_inc(s["pt_ready"], 1)
                    act.wait_ge(s["ot_mm"], h + 1)
                    nc.scalar.activation(halves(b.XT[:, h, :]), b.slot(3)[:, :, 0:HF], ACT.Copy)\
                        .then_inc(s["ot_ready"], 1)

        s = sm
        ring2 = Ring(["act"] * 4 + ["dve"] * 5, {"act": s["act"], "dve": s["dve"]}, 3)
        with nc.Block(no_gpsimd_drain=True) as block:
            @block.sync
            def _(sp):
                for x in [*sa.values(), weights_o]:
                    sp.sem_clear(x)

            @block.vector
            def _(dve):
                c = Chain(dve, s["chain"])
                v = nc.vector
                conditioned_norm_dve(nc, dve, b, c, s)
                for t in range(T):
                    j = KD + t
                    dve.wait_ge(s["mm"], j + 1)
                    v.tensor_tensor(b.V[0:R, t, :], b.RB[0:R, 2 * D:3 * D], b.slot(ring2.slot(j))[0:R, 0, :], ALU.add)\
                        .then_inc(s["dve"], 1)
                    dve.wait_ge(s["dve"], t + 1)
                    v.tensor_tensor(b.H[0:R, t, :], b.H[0:R, t, :], b.V[0:R, t, :], ALU.add).then_inc(s["added"], 1)

            @block.tensor
            def _(pe):
                conditioned_norm_pe(nc, pe, b, s, b.affine[1])
                pe.wait_ge(weights_m, 16)
                for m in range(KD):
                    ring2.acquire(pe, m)
                    matmul_columns(nc, b.slot(ring2.slot(m)), 128, lambda k: M1[:, k, m * 128:(m + 1) * 128],
                                   lambda k: b.XT[:, k, :], KD).then_inc(s["mm"], 1)
                ring2.wait_read(pe, KD - 1)
                for t in range(T):
                    ring2.acquire(pe, KD + t)
                    matmul_rows(nc, b.slot(ring2.slot(KD + t))[0:R, 0, :], lambda k: b.HT[:, k, t * R:(t + 1) * R],
                                lambda k: M2[:, k, :], KD).then_inc(s["mm"], 1)

            @block.scalar
            def _(act):
                layer_norm_act(nc, act, b, s, b.eps5[0:R, :])
                transposes_act(nc, act, b, s, b.XT)
                for m in range(KD):
                    act.wait_ge(s["mm"], m + 1)
                    nc.scalar.activation(halves(b.HT[:, m, :]), b.slot(ring2.slot(m))[:, :, 0:HF], ACT.Relu,
                                         bias=b.lcols[:, 8 + m:9 + m]).then_inc(s["act"], 1)


def add_stream_block(nc, p, b):
    s, = p.sems("stream_added")
    with nc.Block(no_gpsimd_drain=True) as block:
        @block.vector
        def _(dve):
            for t in range(T):
                nc.vector.tensor_tensor(b.X[0:R, t, :], b.X[0:R, t, :], b.H[0:R, t, :], ALU.add).then_inc(s, 1)


def l2_ffn_blocks(nc, p, b, A):
    NE, NG, TG, K, HE, HS = 64, 8, 4, 6, 160, 512
    s = semaphores(p, "f2", "chain", "loaded", "weights", "stats_ready", "std_ready", "xn_ready", "transposed", "xt_ready",
             "logits", "scores", "mm", "silu", "dve", "added")
    bias_bc = b.RB[:, 0:NE]
    sW = [b.W[:, 2048 * i:2048 * (i + 1)].rearrange("p (k n) -> p k n", k=KD) for i in range(3)]
    scores = b.V[0:R, :, 0:NE]
    biased, masked, hot = b.V[0:R, :, 64:128], b.V[0:R, :, 128:192], b.V[0:R, :, 192:256]
    combine = b.combine[0:R, :, :]
    with nc.Block(no_gpsimd_drain=True) as block:
        @block.sync
        def _(sp):
            sp.dma_start(b.router[:, 0:KD * NE], A["L2_ffn_router_w"]).then_inc(s["loaded"], 16)
            sp.dma_start(bias_bc, A["L2_ffn_bias_corr"].partition_broadcast(128)).then_inc(s["loaded"], 16)
            sp.dma_start(b.W[:, 0:6144], A["L2_ffn_sW"]).then_inc(s["weights"], 16)

        @block.tensor
        def _(pe):
            transposes_pe(nc, pe, b, s, b.XN[0:R, :, :], s["xn_ready"])
            pe.wait_ge(s["xt_ready"], T)
            pe.wait_ge(s["loaded"], 32)
            for t in range(T):
                last = matmul_rows(nc, b.ps[0:R, 6, t * NE:(t + 1) * NE], lambda k: b.XT[:, k, t * R:(t + 1) * R],
                                   lambda k: b.router[:, k * NE:(k + 1) * NE], KD)
            last.then_inc(s["logits"], 1)
            pe.wait_ge(s["weights"], 16)
            for j in range(2 * KD):
                if j >= 3:
                    pe.wait_ge(s["dve"], (j - 3) // 2 + 1)
                m = j // 2
                matmul_columns(nc, b.slot(j % 3), 128, lambda k: sW[j % 2][:, k, m * 128:(m + 1) * 128],
                               lambda k: b.XT[:, k, :], KD).then_inc(s["mm"], 1)
            pe.wait_ge(s["dve"], KD)
            for t in range(T):
                matmul_rows(nc, b.ps[0:R, t, :], lambda k: b.HT[:, k, t * R:(t + 1) * R],
                            lambda k: sW[2][:, k, :], KD).then_inc(s["mm"], 1)

        @block.scalar
        def _(act):
            layer_norm_act(nc, act, b, s, b.eps5[0:R, :])
            transposes_act(nc, act, b, s, b.XT)
            act.wait_ge(s["logits"], 1)
            nc.scalar.activation(scores, b.ps[0:R, 6, 0:T * NE].rearrange("p (t e) -> p t e", t=T), ACT.Sigmoid)\
                .then_inc(s["scores"], 1)
            for m in range(KD):
                act.wait_ge(s["mm"], 2 * m + 1)
                nc.scalar.activation(halves(b.HT[:, m, :]), b.slot(2 * m % 3)[:, :, 0:HF], ACT.Silu)\
                    .then_inc(s["silu"], 1)

        @block.vector
        def _(dve):
            c = Chain(dve, s["chain"])
            v = nc.vector
            layer_norm_dve(nc, dve, b, c, s, b.X[0:R, :, :], b.XN[0:R, :, :])
            for m in range(KD):
                dve.wait_ge(s["mm"], 2 * m + 2)
                dve.wait_ge(s["silu"], m + 1)
                v.tensor_tensor(halves(b.HT[:, m, :]), halves(b.HT[:, m, :]), b.slot((2 * m + 1) % 3)[:, :, 0:HF],
                                ALU.mult).then_inc(s["dve"], 1)
            dve.wait_ge(s["scores"], 1)
            c.link(v.tensor_tensor(biased, scores, bias_bc[0:R].unsqueeze(1).to_broadcast([R, T, NE]), ALU.add))
            group = b.gate_tmp[0:R, :, :]
            c.link(v.reduce_max(group, biased.rearrange("p t (g e) -> p t g e", g=NG), AX.X))
            for t in range(T):
                c.mark(v.max(b.top_val[0:R, t, :], group[:, t, :]))
            c.wait()
            for t in range(T):
                c.mark(v.max_index(b.top_idx[0:R, t, :], b.top_val[0:R, t, :], group[:, t, :]))
            c.wait()
            c.link(v.tensor_copy(b.top_idxf[0:R, :, :], b.top_idx[0:R, :, :]))
            gh = b.gate_hot[0:R, :, :]

            def hot_of(out, width, count):
                for k in range(count):
                    for t in range(T):
                        if k == 0:
                            c.mark(v.tensor_scalar(out[:, t, :], b.iota[0:R, 0:width], b.top_idxf[0:R, t, 0:1],
                                                   None, ALU.is_equal))
                        else:
                            c.mark(v.scalar_tensor_tensor(out[:, t, :], b.iota[0:R, 0:width],
                                                          b.top_idxf[0:R, t, k:k + 1], out[:, t, :],
                                                          ALU.is_equal, ALU.add))
                    c.wait()

            hot_of(gh, NG, TG)
            c.link(v.tensor_scalar(group, gh, 1.0, HUGE, ALU.subtract, ALU.mult))
            for t in range(T):
                c.mark(v.tensor_tensor(masked[:, t, :].rearrange("p (g e) -> p g e", g=NG),
                                       biased[:, t, :].rearrange("p (g e) -> p g e", g=NG),
                                       gh[:, t, :].unsqueeze(2).to_broadcast([R, NG, NE // NG]), ALU.mult))
            c.wait()
            for t in range(T):
                c.mark(v.tensor_tensor(masked[:, t, :].rearrange("p (g e) -> p g e", g=NG),
                                       masked[:, t, :].rearrange("p (g e) -> p g e", g=NG),
                                       group[:, t, :].unsqueeze(2).to_broadcast([R, NG, NE // NG]), ALU.add))
            c.wait()
            for t in range(T):
                c.mark(v.max(b.top_val[0:R, t, :], masked[:, t, :]))
            c.wait()
            for t in range(T):
                c.mark(v.max_index(b.top_idx[0:R, t, :], b.top_val[0:R, t, :], masked[:, t, :]))
            c.wait()
            c.link(v.tensor_copy(b.top_idxf[0:R, :, :], b.top_idx[0:R, :, :]))
            hot_of(hot, NE, K)
            c.link(v.tensor_tensor(hot, hot, scores, ALU.mult))
            c.link(v.reduce_sum(b.few[0:R, 0, 0:T], hot, AX.X))
            c.link(v.tensor_scalar(b.few[0:R, 0, 0:T], b.few[0:R, 0, 0:T], 1e-20, None, ALU.add))
            c.link(v.reciprocal(b.few[0:R, 1, 0:T], b.few[0:R, 0, 0:T]))
            c.link(v.tensor_tensor(combine, hot, b.few[0:R, 1, 0:T].unsqueeze(2).to_broadcast([R, T, NE]), ALU.mult))
            for t in range(T):
                dve.wait_ge(s["mm"], 2 * KD + t + 1)
                v.tensor_tensor(b.X[0:R, t, :], b.X[0:R, t, :], b.ps[0:R, t, :], ALU.add).then_inc(s["added"], 1)

    s = semaphores(p, "f2x", "in0", "in1", "gu_mm", "silu", "weighted", "h_ready", "t_mm", "t_ready", "y_mm", "added")
    arrived = [s["in0"], s["in1"]]
    G = 4
    NGR = NE // G
    GW = G * HE
    Wg = [b.W[:, 8192 * u:8192 * u + KD * GW].rearrange("p (k n) -> p k n", k=KD) for u in range(2)]
    Wu = [b.W[:, 8192 * u + KD * GW:8192 * u + 2 * KD * GW].rearrange("p (k n) -> p k n", k=KD) for u in range(2)]
    Wd = [b.W[:, 8192 * u + 2 * KD * GW:8192 * u + 2 * KD * GW + T * D].rearrange("p (k n) -> p k n", k=T)
          for u in range(2)]
    WHALF = 2 * KD * GW + T * D
    HR = [b.QT[0:R, :, :].rearrange("p k n -> p (k n)")[:, GW * i:GW * (i + 1)] for i in range(2)]
    SI = [b.KT[0:R, :, :].rearrange("p k n -> p (k n)")[:, GW * i:GW * (i + 1)] for i in range(2)]
    HTt = [b.HT[:, :, :].rearrange("p k n -> p (k n)")[:, 640 * i:640 * (i + 1)].rearrange("p (c n) -> p c n", c=5)
           for i in range(2)]
    GH = GW // 2
    with nc.Block(no_gpsimd_drain=True) as block:
        @block.sync
        def _(sp):
            def load(i, u, first):
                if not first:
                    sp.wait_ge(s["y_mm"], (i - 1) * 2 * T + T * (u + 1))
                g = i * 2 + u
                sp.dma_start(b.W[:, 8192 * u:8192 * u + WHALF],
                             A["L2_ffn_experts"][bass.ds(g, 1), :, :].rearrange("a p n -> p (a n)"))\
                    .then_inc(arrived[u], 16)

            for u in range(2):
                load(0, u, True)
            with sp.Fori(1, NGR // 2) as i:
                for u in range(2):
                    load(i, u, False)

        @block.tensor
        def _(pe):
            def turn(i, first):
                for u in range(2):
                    pe.wait_ge(arrived[u], 16 * (i + 1))
                    for t in range(T + 1):
                        if t < T:
                            for a in range(2):
                                n = ((i * 2 + u) * T + t) * 2 + a
                                if not (first and u == 0 and t == 0):
                                    pe.wait_ge(s["weighted"], n - 1)
                                for w, bank in ((Wg, 2 * a), (Wu, 2 * a + 1)):
                                    last = matmul_rows(nc, b.ps[0:R, bank, 0:GH],
                                                       lambda k: b.XT[:, k, t * R:(t + 1) * R],
                                                       lambda k: w[u][:, k, a * GH:(a + 1) * GH], KD)
                                last.then_inc(s["gu_mm"], 1)
                        if t:
                            n = (i * 2 + u) * T + t - 1
                            pe.wait_ge(s["weighted"], 2 * n + 2)
                            wait_positive(pe, s["t_ready"], 2 * n)
                            for q in range(5):
                                last = nc.tensor.transpose(b.ps[:, 4 + q // 4, (q % 4) * 128:(q % 4) * 128 + R],
                                                           HR[(t - 1) % 2][:, q * 128:(q + 1) * 128],
                                                           b.ident[0:R, 0:R])
                            last.then_inc(s["t_mm"], 1)
                            pe.wait_ge(s["t_ready"], 2 * n + 2)
                            wait_positive(pe, s["added"], n - 1)
                            matmul_rows(nc, b.ps[0:R, 6 + (u * T + t - 1) % 2, :],
                                        lambda k: HTt[(t - 1) % 2][:, k, 0:R], lambda k: Wd[u][:, k, :], 5)\
                                .then_inc(s["y_mm"], 1)

            turn(0, True)
            with pe.Fori(1, NGR // 2) as i:
                turn(i, False)

        @block.scalar
        def _(act):
            def turn(i, first):
                for u in range(2):
                    for t in range(T + 1):
                        if t < T:
                            for a in range(2):
                                n = ((i * 2 + u) * T + t) * 2 + a
                                act.wait_ge(s["gu_mm"], n + 1)
                                if not (first and u == 0 and t < 2):
                                    act.wait_ge(s["weighted"], n - 3)
                                nc.scalar.activation(SI[t % 2][:, a * GH:(a + 1) * GH], b.ps[0:R, 2 * a, 0:GH],
                                                     ACT.Silu).then_inc(s["silu"], 1)
                        if t:
                            n = (i * 2 + u) * T + t - 1
                            act.wait_ge(s["t_mm"], n + 1)
                            if not (first and u == 0 and t <= 2):
                                act.wait_ge(s["y_mm"], n - 1)
                            nc.scalar.activation(HTt[(t - 1) % 2][:, 0:4, 0:R],
                                                 b.ps[:, 4, :].rearrange("p (q n) -> p q n", q=4)[:, :, 0:R],
                                                 ACT.Copy).then_inc(s["t_ready"], 1)
                            nc.scalar.activation(HTt[(t - 1) % 2][:, 4, 0:R], b.ps[:, 5, 0:R], ACT.Copy)\
                                .then_inc(s["t_ready"], 1)

            turn(0, True)
            with act.Fori(1, NGR // 2) as i:
                turn(i, False)

        @block.vector
        def _(dve):
            v = nc.vector

            def turn(i, first):
                for u in range(2):
                    for t in range(T + 1):
                        if t < T:
                            for a in range(2):
                                n = ((i * 2 + u) * T + t) * 2 + a
                                dve.wait_ge(s["silu"], n + 1)
                                if not (first and u == 0 and t < 2):
                                    dve.wait_ge(s["t_mm"], (i * 2 + u) * T + t - 1)
                                for e in range(2):
                                    cols = slice(a * GH + e * HE, a * GH + (e + 1) * HE)
                                    ins = v.scalar_tensor_tensor(
                                        HR[t % 2][:, cols], b.ps[0:R, 2 * a + 1, e * HE:(e + 1) * HE],
                                        combine[:, t, bass.ds((i * 2 + u) * G + 2 * a + e, 1)], SI[t % 2][:, cols],
                                        ALU.mult, ALU.mult)
                                ins.then_inc(s["weighted"], 1)
                        if t:
                            n = (i * 2 + u) * T + t - 1
                            dve.wait_ge(s["y_mm"], n + 1)
                            if not (first and u == 0):
                                dve.wait_ge(s["added"], n - T + 1)
                            v.tensor_tensor(b.X[0:R, t - 1, :], b.X[0:R, t - 1, :],
                                            b.ps[0:R, 6 + (u * T + t - 1) % 2, :], ALU.add).then_inc(s["added"], 1)

            turn(0, True)
            with dve.Fori(1, NGR // 2) as i:
                turn(i, False)


def l3_gnn_block(nc, p, b, A):
    s = semaphores(p, "g3", "chain", "loaded", "stats_ready", "std_ready", "xn_ready", "transposed", "xt_ready", "deg_mm",
             "agg_mm", "agg_ready", "mm", "read")
    W1 = b.W[:, 0:2048].rearrange("p (k n) -> p k n", k=KD)
    W2 = b.W[:, 2048:4096].rearrange("p (k n) -> p k n", k=KD)
    with nc.Block(no_gpsimd_drain=True) as block:
        @block.sync
        def _(sp):
            sp.dma_start(b.W[:, 0:4096], A["L3_gnn_W12"]).then_inc(s["loaded"], 16)
            sp.dma_start(b.RB[:, 0:1024], A["L3_gnn_b12"].partition_broadcast(128)).then_inc(s["loaded"], 16)

        @block.tensor
        def _(pe):
            for t in range(T):
                for k in range(T):
                    last = nc.tensor.matmul(b.ps[0:R, 5, t:t + 1], b.CNT[0:R, k, t * R:(t + 1) * R],
                                            b.ones[0:R, 0:1], start=(k == 0), stop=(k == T - 1))
            last.then_inc(s["deg_mm"], 1)
            transposes_pe(nc, pe, b, s, b.XN[0:R, :, :], s["xn_ready"])
            for m in range(KD):
                if m >= 2:
                    pe.wait_ge(s["agg_ready"], m - 1)
                matmul_columns(nc, b.slot(m % 2), 128, lambda k: b.XN[0:R, k, m * 128:(m + 1) * 128],
                               lambda k: b.CNT[0:R, k, :], T).then_inc(s["agg_mm"], 1)
            pe.wait_ge(s["xt_ready"], T)
            pe.wait_ge(s["agg_ready"], KD)
            pe.wait_ge(s["loaded"], 32)
            for t in range(T):
                if t >= 2:
                    pe.wait_ge(s["read"], t - 1)
                matmul_rows(nc, b.ps[0:R, 2 * (t % 2), :], lambda k: b.XT[:, k, t * R:(t + 1) * R],
                            lambda k: W1[:, k, :], KD)
                matmul_rows(nc, b.ps[0:R, 2 * (t % 2) + 1, :], lambda k: b.QT[:, k, t * R:(t + 1) * R],
                            lambda k: W2[:, k, :], KD).then_inc(s["mm"], 1)

        @block.scalar
        def _(act):
            layer_norm_act(nc, act, b, s, b.eps5[0:R, :])
            transposes_act(nc, act, b, s, b.XT)
            for m in range(KD):
                act.wait_ge(s["agg_mm"], m + 1)
                nc.scalar.activation(halves(b.QT[:, m, :]), b.slot(m % 2)[:, :, 0:HF], ACT.Copy)\
                    .then_inc(s["agg_ready"], 1)

        @block.vector
        def _(dve):
            c = Chain(dve, s["chain"])
            v = nc.vector
            layer_norm_dve(nc, dve, b, c, s, b.X[0:R, :, :], b.XN[0:R, :, :])
            dve.wait_ge(s["deg_mm"], 1)
            c.link(v.tensor_scalar(b.few[0:R, 0, 0:T], b.ps[0:R, 5, 0:T], 1.0, None, ALU.max))
            c.link(v.reciprocal(b.few[0:R, 1, 0:T], b.few[0:R, 0, 0:T]))
            dve.wait_ge(s["loaded"], 32)
            c.link(v.tensor_tensor(b.RB[:, 0:D], b.RB[:, 0:D], b.RB[:, D:2 * D], ALU.add))
            for t in range(T):
                c.mark(v.tensor_tensor(b.H[0:R, t, :], b.X[0:R, t, :], b.RB[0:R, 0:D], ALU.add))
            c.wait()
            for t in range(T):
                dve.wait_ge(s["mm"], t + 1)
                c.link(v.tensor_tensor(b.H[0:R, t, :], b.H[0:R, t, :], b.ps[0:R, 2 * (t % 2), :], ALU.add))
                v.scalar_tensor_tensor(b.X[0:R, t, :], b.ps[0:R, 2 * (t % 2) + 1, :], b.few[0:R, 1, t:t + 1],
                                       b.H[0:R, t, :], ALU.mult, ALU.add).then_inc(s["read"], 1)


def l3_ffn_blocks(nc, p, b, A, out):
    NE, H2 = 8, 2 * D // 128
    s = semaphores(p, "f3", "chain", "loaded", "stats_ready", "std_ready", "xn_ready", "transposed", "xt_ready", "logits",
             "logits_shifted", "gates_exp", "gates_ready", "gates_t", "gt_ready", "b2_mm", "b2_added")
    with nc.Block(no_gpsimd_drain=True) as block:
        @block.sync
        def _(sp):
            sp.dma_start(b.router[:, 0:KD * NE], A["L3_ffn_gate_w"]).then_inc(s["loaded"], 16)
            sp.dma_start(b.RB[:, 0:NE], A["L3_ffn_gate_b"].partition_broadcast(128)).then_inc(s["loaded"], 16)
            sp.dma_start(b.RB[0:NE, 512:1024], A["L3_ffn_b2"]).then_inc(s["loaded"], 16)

        @block.tensor
        def _(pe):
            transposes_pe(nc, pe, b, s, b.XN[0:R, :, :], s["xn_ready"])
            pe.wait_ge(s["xt_ready"], T)
            pe.wait_ge(s["loaded"], 48)
            for t in range(T):
                last = matmul_rows(nc, b.ps[0:R, 5, t * NE:(t + 1) * NE], lambda k: b.XT[:, k, t * R:(t + 1) * R],
                                   lambda k: b.router[:, k * NE:(k + 1) * NE], KD)
            last.then_inc(s["logits"], 1)
            pe.wait_ge(s["gates_ready"], 1)
            for t in range(T):
                last = nc.tensor.transpose(b.ps[0:8, 6 + t // 4, (t % 4) * 128:(t % 4) * 128 + R],
                                           b.gates[0:R, t, 0:8], b.ident[0:R, 0:R])
            last.then_inc(s["gates_t"], 1)
            pe.wait_ge(s["gt_ready"], 2)
            for t in range(T):
                nc.tensor.matmul(b.ps[0:R, t, :], b.GT[0:NE, t * R:(t + 1) * R], b.RB[0:NE, 512:1024],
                                 start=True, stop=True).then_inc(s["b2_mm"], 1)

        @block.scalar
        def _(act):
            layer_norm_act(nc, act, b, s, b.eps5[0:R, :])
            transposes_act(nc, act, b, s, b.XT)
            experts_top2_act(nc, act, b, s)
            act.wait_ge(s["gates_t"], 1)
            gt = b.GT[0:8, 0:4 * R].rearrange("p (t n) -> p t n", t=4)
            nc.scalar.activation(gt, b.ps[0:8, 6, :].rearrange("p (t n) -> p t n", t=4)[:, :, 0:R], ACT.Copy)\
                .then_inc(s["gt_ready"], 1)
            nc.scalar.activation(b.GT[0:8, 4 * R:N], b.ps[0:8, 7, 0:R], ACT.Copy).then_inc(s["gt_ready"], 1)

        @block.vector
        def _(dve):
            c = Chain(dve, s["chain"])
            v = nc.vector
            layer_norm_dve(nc, dve, b, c, s, b.X[0:R, :, :], b.XN[0:R, :, :])
            dve.wait_ge(s["loaded"], 48)
            dve.wait_ge(s["logits"], 1)
            c.link(v.tensor_tensor(b.logits[0:R, :, 0:NE], b.ps[0:R, 5, 0:T * NE].rearrange("p (t e) -> p t e", t=T),
                                   b.RB[0:R, 0:NE].unsqueeze(1).to_broadcast([R, T, NE]), ALU.add))
            experts_top2(nc, dve, None, c, b, b.logits[0:R, :, 0:8], b.gates[0:R, :, 0:8], s, 0)
            for t in range(T):
                dve.wait_ge(s["b2_mm"], t + 1)
                v.tensor_tensor(b.X[0:R, t, :], b.X[0:R, t, :], b.ps[0:R, t, :], ALU.add).then_inc(s["b2_added"], 1)

    s = semaphores(p, "f3x", "w_in0", "w_in1", "b_in0", "b_in1", "hidden_mm", "hidden_ready", "y_mm", "added", "stored")
    arrived = [s["w_in0"], s["w_in1"]]
    W1 = [b.W[:, 8192 * u:8192 * u + 4096].rearrange("p (k n) -> p k n", k=KD) for u in range(2)]
    W2 = [b.W[:, 8192 * u + 4096:8192 * (u + 1)].rearrange("p (k n) -> p k n", k=H2) for u in range(2)]
    bias = [b.lcols[:, 0:8], b.lcols[:, 8:16]]
    with nc.Block(no_gpsimd_drain=True) as block:
        @block.sync
        def _(sp):
            def load(i, u, first):
                e = i * 2 + u
                if not first:
                    sp.wait_ge(s["y_mm"], (i - 1) * 2 * T + T * (u + 1))
                sp.dma_start(b.W[:, 8192 * u:8192 * (u + 1)],
                             A["L3_ffn_w12"][bass.ds(e, 1), :, :].rearrange("a p n -> p (a n)")).then_inc(arrived[u], 16)
                sp.dma_start(bias[u], A["L3_ffn_b1"][bass.ds(e, 1), :, :].rearrange("a p n -> p (a n)"))\
                    .then_inc(arrived[u], 16)

            for u in range(2):
                load(0, u, True)
            with sp.Fori(1, NE // 2) as i:
                for u in range(2):
                    load(i, u, False)
            sp.wait_ge(s["added"], NE * T)
            sp.dma_start(out.rearrange("p (t d) -> p t d", t=T), b.X[0:R, :, :]).then_inc(s["stored"], 16)
            sp.wait_ge(s["stored"], 16)

        @block.tensor
        def _(pe):
            def turn(i, first):
                for u in range(2):
                    pe.wait_ge(arrived[u], 32 * (i + 1))
                    for m in range(H2):
                        n = (i * 2 + u) * H2 + m
                        if not (first and u == 0 and m < 2):
                            pe.wait_ge(s["hidden_ready"], n - 1)
                        matmul_columns(nc, b.slot(m % 2), 128, lambda k: W1[u][:, k, m * 128:(m + 1) * 128],
                                       lambda k: b.XT[:, k, :], KD).then_inc(s["hidden_mm"], 1)
                    pe.wait_ge(s["hidden_ready"], (i * 2 + u + 1) * H2)
                    for t in range(T):
                        n = (i * 2 + u) * T + t
                        if t == 0 and not (first and u == 0):
                            pe.wait_ge(s["added"], n)
                        elif t == 4:
                            pe.wait_ge(s["added"], n - 3)
                        matmul_rows(nc, b.ps[0:R, 4 + t % 4, :],
                                    lambda k: b.HT[:, k, t * R:(t + 1) * R], lambda k: W2[u][:, k, :], H2)\
                            .then_inc(s["y_mm"], 1)

            turn(0, True)
            with pe.Fori(1, NE // 2) as i:
                turn(i, False)

        @block.scalar
        def _(act):
            def turn(i, first):
                for u in range(2):
                    act.wait_ge(arrived[u], 32 * (i + 1))
                    for m in range(H2):
                        n = (i * 2 + u) * H2 + m
                        act.wait_ge(s["hidden_mm"], n + 1)
                        if not (first and u == 0):
                            act.wait_ge(s["y_mm"], (i * 2 + u) * T)
                        nc.scalar.activation(halves(b.HT[:, m, :]), b.slot(m % 2)[:, :, 0:HF], ACT.Relu,
                                             bias=bias[u][:, m:m + 1]).then_inc(s["hidden_ready"], 1)

            turn(0, True)
            with act.Fori(1, NE // 2) as i:
                turn(i, False)

        @block.vector
        def _(dve):
            def turn(i, first):
                for u in range(2):
                    for t in range(T):
                        n = (i * 2 + u) * T + t
                        dve.wait_ge(s["y_mm"], n + 1)
                        if not (first and u == 0):
                            dve.wait_ge(s["added"], n - T + 1)
                        nc.vector.scalar_tensor_tensor(
                            b.X[0:R, t, :], b.ps[0:R, 4 + t % 4, :], b.gates[0:R, t, bass.ds(i * 2 + u, 1)],
                            b.X[0:R, t, :], ALU.mult, ALU.add).then_inc(s["added"], 1)

            turn(0, True)
            with dve.Fori(1, NE // 2) as i:
                turn(i, False)


_COLS = [("b1", 8), ("g1", 8), ("be1", 8), ("b2", 4), ("g2", 4), ("be2", 4), ("f0b1", 8), ("freq", 1),
         ("f_b1", 1), ("f_b2", 1)]


def build(nc, A, out, table, hb):
    ctx = ExitStack()
    with ctx:
        p = Program(nc, ctx, A)
        b = Buffers()
        sb = p.sb
        b.ps = ctx.enter_context(nc.psum_tensor("ps", [128, 8, 512], F32))
        b.slot = lambda j: b.ps[:, 2 * j:2 * j + 2, :]
        b.X = sb("X", [128, T, D])
        b.XN = sb("XN", [128, T, D])
        b.H = sb("H", [128, T, D])
        b.V = sb("V", [128, T, D])
        b.XT = sb("XT", [128, KD, NP])
        b.HT = sb("HT", [128, 8, NP])
        b.QT = sb("QT", [128, KD, NP])
        b.KT = sb("KT", [128, KD, NP])
        b.CNT = sb("CNT", [128, T, NP])
        b.LOGC = sb("LOGC", [128, T, NP])
        b.P = sb("P", [128, T, NP])
        b.W = sb("W", [128, 16384])
        b.RB = sb("RB", [128, 2048])
        b.ident = sb("ident", [128, 128])
        b.ones = sb("ones", [128, 128])
        b.iota = sb("iota", [128, NP])
        b.iota_int = b.V[:, 0:2, :].rearrange("p a n -> p (a n)")[:, 0:NP].bitcast(I32)
        b.idx_int = b.V[:, 2, 0:2 * EC].bitcast(I32).rearrange("p (a n) -> p a n", a=2)
        b.eid_int = b.V[:, 3, 0:EC].bitcast(I32)
        b.cols = sb("cols", [128, sum(n for _, n in _COLS)])
        b.col_of, at = {}, 0
        for name, n in _COLS:
            b.col_of[name] = at
            at += n
        b.lcols = sb("lcols", [128, 16])
        b.eps5, b.eps6, b.half_pi = sb("eps5", [128, 1]), sb("eps6", [128, 1]), sb("half_pi", [128, 1])
        b.eps_col = sb("eps_col", [128, 1])
        b.stats, b.mv, b.mv2 = sb("stats", [128, T, 6]), sb("mv", [128, T, 2]), sb("mv2", [128, 2, T, 2])
        b.var, b.std, b.rstd = sb("var", [128, 8]), sb("std", [128, 8]), sb("rstd", [128, 8])
        b.aff = sb("aff", [128, 2, 2, T])
        b.bn_st, b.bn_mv = sb("bn_st", [128, 8, 2, 6]), sb("bn_mv", [128, 8, 2])
        b.bn_var, b.bn_std = sb("bn_var", [128, 8]), sb("bn_std", [128, 8])
        b.bn_scale, b.bn_bias = sb("bn_scale", [128, 8]), sb("bn_bias", [128, 8])
        b.router = b.RB[:, 1536:1792]
        b.logits, b.gates = sb("logits", [128, T, 8]), sb("gates", [128, T, 8])
        b.gate_tmp, b.gate_hot = sb("gate_tmp", [128, T, 8]), sb("gate_hot", [128, T, 8])
        b.top_val, b.top_idx, b.top_idxf = (sb("top_val", [128, T, 8]), sb("top_idx", [128, T, 8], U32),
                                            sb("top_idxf", [128, T, 8]))
        b.combine = b.RB[:, 512:832].rearrange("p (t e) -> p t e", t=T)
        b.GT = sb("GT", [128, NP])
        b.few, b.few_int = sb("few", [128, 5, T]), sb("few_int", [128, 2, T], I32)
        b.row_has = sb("row_has", [128, T])
        b.smax, b.nmax, b.den = sb("smax", [128, 20]), sb("nmax", [128, 20]), sb("den", [128, 20])
        b.gather_idx = [sb(f"gather_idx{u}", [128, 1], I32) for u in range(SLOT_UNROLL)]
        qt, kt = (x[:, :, :].rearrange("p k n -> p (k n)") for x in (b.QT, b.KT))
        b.gathered = [qt[:, 512 * u:512 * (u + 1)] for u in range(SLOT_UNROLL)]
        b.message = [kt[:, 512 * u:512 * (u + 1)] for u in range(SLOT_UNROLL)]
        pf, lf = (x[:, :, :].rearrange("p t n -> p (t n)") for x in (b.P, b.LOGC))
        b.hot = [pf[:, 128 * u:128 * u + R] for u in range(SLOT_UNROLL)]
        b.attr = [pf[:, 512 + 128 * u:640 + 128 * u] for u in range(SLOT_UNROLL)]
        b.tri, b.eid, b.place = lf[:, 0:128], lf[:, 128:128 + EC], lf[:, 256:256 + EC].bitcast(I32)
        b.slot_src, b.slot_edge, b.slot_off = (lf[:, 512 + 128 * i:512 + 128 * i + NSLOT].bitcast(I32) for i in range(3))
        b.slot_dst = lf[:, 896:896 + NSLOT]
        b.idx = lf[:, 1024:1024 + 2 * EC].rearrange("p (a j) -> p a j", a=2)
        b.EAT = b.W[:, 0:NSLOT * 128]
        ht = b.HT[:, :, :].rearrange("p k n -> p (k n)")
        b.PT = ht[:, 0:T * NP].rearrange("p (t n) -> p t n", t=T)
        b.affine = [ht[0:17, 0:2 * D], ht[0:17, 3200:3200 + 2 * D]]
        at = [0]

        def take(n):
            at[0] += n
            return ht[:, at[0] - n:at[0]]

        b.src_hot = take(4 * 375 // 2).bitcast(BF16).rearrange("p (u n) -> p u n", u=4)
        b.dst_hot = take(4 * NP // 2).bitcast(BF16).rearrange("p (u n) -> p u n", u=4)
        at[0] = 0
        b.tile_ge, b.tile_hot, b.scan_a, b.scan_b = (take(T * EC).rearrange("p (k j) -> p k j", k=T)
                                                     for _ in range(4))
        b.slot_init, b.slot_tab = (take(NSLOT * 4).rearrange("p (t c) -> p t c", c=4) for _ in range(2))
        b.payload = take(EC * 4).rearrange("p (j c) -> p j c", c=4)
        b.slot_tmp = take(EC).rearrange("p (a j) -> p a j", a=1)
        b.slot_tile = take(NSLOT)

        setup_block(nc, p, b, A)
        count_block(nc, p, b, A)
        slots_block(nc, p, b, A, table)
        l0_gnn_block(nc, p, b, A)
        l0_ffn_block(nc, p, b, A)
        release_semaphores(nc, p)
        attributes_block(nc, p, b, A)
        l1_gnn_blocks(nc, p, b, A, hb)
        release_semaphores(nc, p)
        l1_ffn_blocks(nc, p, b, A)
        release_semaphores(nc, p)
        l2_start_block(nc, p, b, A)
        l2_gnn_blocks(nc, p, b, A)
        add_stream_block(nc, p, b)
        release_semaphores(nc, p)
        l2_ffn_blocks(nc, p, b, A)
        release_semaphores(nc, p)
        l3_gnn_block(nc, p, b, A)
        l3_ffn_blocks(nc, p, b, A, out)


def _layout(inputs):
    import numpy as np
    a = {k: np.asarray(v) for k, v in inputs.items()}
    f = np.float32

    def rows(x):
        k = x.shape[0] // 128
        return x.reshape(k, 128, -1).transpose(1, 0, 2).reshape(128, -1)

    def col(x):
        return x.reshape(-1, 128).T

    def pad(x):
        out = np.zeros((128, 1), f)
        out[:len(x), 0] = x
        return out

    freq = pad(np.tile(np.arange(1, 33, dtype=f) * f(TWO_PI / 16), 2))
    cols = [col(a["L0_gnn_b1"]), col(a["L0_gnn_g1"]), col(a["L0_gnn_be1"]), col(a["L0_gnn_b2"]), col(a["L0_gnn_g2"]),
            col(a["L0_gnn_be2"]), a["L0_ffn_b1"].T, freq, pad(a["L2_gnn_f_b1"]), pad(a["L2_gnn_f_b2"])]
    out = {
        "x": a["x"].reshape(T, R, D).transpose(1, 0, 2).reshape(R, T * D),
        "src": a["src"].reshape(R, EC), "dst": a["dst"].reshape(R, EC),
        "edge_attr_128": a["edge_attr_128"], "node_vec1": a["node_vec1"].reshape(-1),
        "cols": np.concatenate(cols, axis=1),
        "L0_gnn_eps": a["L0_gnn_eps"].reshape(1), "L0_gnn_W1": rows(a["L0_gnn_W1"]), "L0_gnn_W2": rows(a["L0_gnn_W2"]),
        "L0_ffn_router_w": rows(a["L0_ffn_router_w"]), "L0_ffn_beta": a["L0_ffn_beta"],
        "L0_ffn_b2": a["L0_ffn_b2"].reshape(1, -1), "L0_ffn_gamma": a["L0_ffn_gamma"].reshape(-1),
        "L0_ffn_w1": np.concatenate([rows(w) for w in a["L0_ffn_w1"]], axis=1),
        "L0_ffn_w2": np.concatenate(list(a["L0_ffn_w2"]), axis=1),
        "L1_gnn_rows": np.concatenate([a["L1_gnn_be"], a["L1_gnn_b2"], a["L1_gnn_gamma"], a["L1_gnn_beta"]], axis=1),
        "L1_gnn_eps": a["L1_gnn_eps"], "L1_gnn_We": a["L1_gnn_We"],
        "L1_gnn_W12": np.stack([np.concatenate([rows(a["L1_gnn_W1"][i]), rows(a["L1_gnn_W2"][i])], axis=1)
                                for i in range(3)]),
        "L1_gnn_b1": np.stack([col(x) for x in a["L1_gnn_b1"]]),
        "L1_gnn_Wf": rows(a["L1_gnn_Wf"]), "L1_gnn_bf": a["L1_gnn_bf"],
        "L1_ffn_w_gating": rows(a["L1_ffn_w_gating"]), "L1_ffn_gamma": a["L1_ffn_gamma"],
        "L1_ffn_w1": np.concatenate([rows(w) for w in a["L1_ffn_w1"]], axis=1),
        "L1_ffn_w2": np.concatenate(list(a["L1_ffn_w2"]), axis=1),
        "L2_gnn_f_w1": a["L2_gnn_f_w1"], "L2_gnn_f_w2": a["L2_gnn_f_w2"],
        "L2_gnn_sb": np.concatenate([np.concatenate([a[f"L2_gnn_{n}_w"], a[f"L2_gnn_{n}_b"][:, None, :]], axis=1)
                                     for n in ("s1", "b1", "s2", "b2")], axis=2),
        "L2_gnn_Wqkv": np.stack([np.concatenate([rows(a[f"L2_gnn_w{n}"][i]) for n in "qkv"], axis=1)
                                 for i in range(4)]),
        "L2_gnn_cols": np.stack([np.concatenate([col(a[f"L2_gnn_{n}"][i]) for n in ("bq", "bk", "m_b1")], axis=1)
                                 for i in range(4)]),
        "L2_gnn_rows": np.concatenate([a["L2_gnn_bv"], a["L2_gnn_bo"], a["L2_gnn_m_b2"]], axis=1),
        "L2_gnn_wo": np.stack([rows(w) for w in a["L2_gnn_wo"]]),
        "L2_gnn_Wm": np.stack([np.concatenate([rows(a["L2_gnn_m_w1"][i]), rows(a["L2_gnn_m_w2"][i])], axis=1)
                               for i in range(4)]),
        "L2_ffn_router_w": rows(a["L2_ffn_router_w"].T), "L2_ffn_bias_corr": a["L2_ffn_bias_corr"],
        "L2_ffn_sW": np.concatenate([rows(a[f"L2_ffn_{n}"]) for n in ("sWg", "sWu", "sWd")], axis=1),
        "L3_gnn_W12": np.concatenate([rows(a["L3_gnn_W1"].T), rows(a["L3_gnn_W2"].T)], axis=1),
        "L3_gnn_b12": np.concatenate([a["L3_gnn_b1"], a["L3_gnn_b2"]]),
        "L3_ffn_gate_w": rows(a["L3_ffn_gate_w"]), "L3_ffn_gate_b": a["L3_ffn_gate_b"], "L3_ffn_b2": a["L3_ffn_b2"],
        "L3_ffn_w12": np.stack([np.concatenate([rows(a["L3_ffn_w1"][e]), rows(a["L3_ffn_w2"][e])], axis=1)
                                for e in range(8)]),
        "L3_ffn_b1": np.stack([col(x) for x in a["L3_ffn_b1"]]),
    }
    groups = []
    for g in range(16):
        e = range(4 * g, 4 * g + 4)
        groups.append(np.concatenate(
            [rows(np.concatenate([a["L2_ffn_Wg"][i] for i in e], axis=1)),
             rows(np.concatenate([a["L2_ffn_Wu"][i] for i in e], axis=1)),
             rows(np.concatenate([a["L2_ffn_Wd"][i] for i in e], axis=0))], axis=1))
    out["L2_ffn_experts"] = np.stack(groups)
    return {k: np.ascontiguousarray(v) for k, v in out.items()}


def kernel(**inputs):
    import numpy as np
    import concourse.bacc as bacc
    from concourse.bass_utils import run_bass_kernel_spmd
    nc = bacc.Bacc("TRN2", target_bir_lowering=False, num_devices=1)
    arrays = {f"in_{k}": v for k, v in _layout(inputs).items()}
    A = {k[3:]: nc.dram_tensor(k, v.shape, mybir.dt.from_np(v.dtype), kind="ExternalInput").ap()
         for k, v in arrays.items()}
    out = nc.dram_tensor("out", (R, T * D), F32, kind="ExternalOutput").ap()
    table = nc.dram_tensor("slot_table", (NSLOT * 128, 4), F32).ap()
    hb = nc.dram_tensor("node_rows", (N, D), F32).ap()
    build(nc, A, out, table, hb)
    r = run_bass_kernel_spmd(nc, [arrays], core_ids=[0])
    got = np.asarray(r.results[0]["out"])
    return got.reshape(R, T, D).transpose(1, 0, 2).reshape(N, D)
```
